# Optimizing a Trainium2 kernel written in Bass

```python
import numpy as np
import jax
import jax.numpy as jnp

def _softmax(x, axis=-1):
    return jax.nn.softmax(x, axis=axis)

def _gelu(x):
    return jax.nn.gelu(x, approximate=True)

def _silu(x):
    return jax.nn.silu(x)

def _sigmoid(x):
    return jax.nn.sigmoid(x)

def _layernorm(x, axis=-1, eps=1e-05):
    m = jnp.mean(x, axis=axis, keepdims=True)
    v = jnp.var(x, axis=axis, keepdims=True)
    return (x - m) / jnp.sqrt(v + eps)

def _scatter_add(tgt, idx, src, axis=0):
    return tgt.at[idx].add(src)

def _segment_sum(src, seg, n):
    return jax.ops.segment_sum(src, seg, n)
kernel_name = 'mk_prb_d1_jaxref_r4_f0b2d7'

def setup_inputs(seed: int=0):
    np.random.seed(seed)
    _w = jnp.asarray

    def _L0_attn_setup():
        import jax, jax.numpy as jnp
        import numpy as np
        B, T, D, N = (8, 512, 256, 64)
        key = jax.random.key(seed)
        ks = jax.random.split(key, 6)
        sD = 1.0 / np.sqrt(D)
        sN = 1.0 / np.sqrt(N)
        return {'x': jax.random.normal(ks[0], (B, T, D), dtype=jnp.float32), 'Wa': jax.random.normal(ks[1], (D, N), dtype=jnp.float32) * sD, 'ba': jnp.zeros((N,), jnp.float32), 'Wb': jax.random.normal(ks[2], (D, N), dtype=jnp.float32) * sD, 'bb': jnp.zeros((N,), jnp.float32), 'Wc': jax.random.normal(ks[3], (D, N), dtype=jnp.float32) * sD, 'bc': jnp.zeros((N,), jnp.float32), 'Wd': jax.random.normal(ks[4], (D, D), dtype=jnp.float32) * sD, 'bd': jnp.zeros((D,), jnp.float32), 'Wy': jax.random.normal(ks[5], (N, D), dtype=jnp.float32) * sN, 'by': jnp.zeros((D,), jnp.float32)}
    _L0_attn_in = _L0_attn_setup()

    def _L0_ffn_setup():
        import jax, jax.numpy as jnp
        import numpy as np
        E = 8
        K = 2
        C = 256
        F = 512
        EPS = 1e-05
        key = jax.random.key(seed)
        ks = jax.random.split(key, 6)
        x = jax.random.normal(ks[0], (2, 256, C), dtype=jnp.float32)
        ln_gamma = 1.0 + 0.02 * jax.random.normal(ks[1], (C,), dtype=jnp.float32)
        ln_beta = 0.02 * jax.random.normal(ks[2], (C,), dtype=jnp.float32)
        gate_w = jax.random.normal(ks[3], (E, C), dtype=jnp.float32) / np.sqrt(C)
        w1 = jax.random.normal(ks[4], (E, F, C), dtype=jnp.float32) / np.sqrt(C)
        w2 = jax.random.normal(ks[5], (E, C, F), dtype=jnp.float32) / np.sqrt(F)
        return {'x': x, 'ln_gamma': ln_gamma, 'ln_beta': ln_beta, 'gate_w': gate_w, 'w1': w1, 'w2': w2}
    _L0_ffn_in = _L0_ffn_setup()
    _d = {'L0_attn_x': _L0_attn_in['x'], 'L0_attn_Wa': _L0_attn_in['Wa'], 'L0_attn_ba': _L0_attn_in['ba'], 'L0_attn_Wb': _L0_attn_in['Wb'], 'L0_attn_bb': _L0_attn_in['bb'], 'L0_attn_Wc': _L0_attn_in['Wc'], 'L0_attn_bc': _L0_attn_in['bc'], 'L0_attn_Wd': _L0_attn_in['Wd'], 'L0_attn_bd': _L0_attn_in['bd'], 'L0_attn_Wy': _L0_attn_in['Wy'], 'L0_attn_by': _L0_attn_in['by'], 'L0_ffn_ln_gamma': _L0_ffn_in['ln_gamma'], 'L0_ffn_ln_beta': _L0_ffn_in['ln_beta'], 'L0_ffn_gate_w': _L0_ffn_in['gate_w'], 'L0_ffn_w1': _L0_ffn_in['w1'], 'L0_ffn_w2': _L0_ffn_in['w2']}
    _x0 = _d['L0_attn_x']
    _d['L0_attn_x'] = jax.random.normal(jax.random.fold_in(jax.random.key(seed), 1), (4, 2048, 256), dtype=_x0.dtype)
    del _x0
    return _d

def reference(L0_attn_x, L0_attn_Wa, L0_attn_ba, L0_attn_Wb, L0_attn_bb, L0_attn_Wc, L0_attn_bc, L0_attn_Wd, L0_attn_bd, L0_attn_Wy, L0_attn_by, L0_ffn_ln_gamma, L0_ffn_ln_beta, L0_ffn_gate_w, L0_ffn_w1, L0_ffn_w2):

    def _L0_attn_ref(x, Wa, ba, Wb, bb, Wc, bc, Wd, bd, Wy, by):
        import jax, jax.numpy as jnp
        import numpy as np
        B, T, D, N = (8, 512, 256, 64)
        a = jax.nn.sigmoid(jnp.einsum('btd,dn->btn', x, Wa) + ba)
        b = jnp.einsum('btd,dn->btn', x, Wb) + bb
        c = jnp.tanh(jnp.einsum('btd,dn->btn', x, Wc) + bc)
        d = jnp.einsum('btd,de->bte', x, Wd) + bd

        def step(s, abc):
            at, bt, ct = abc
            s = at * s + (1.0 - at) * bt
            return (s, ct * s)
        aT = jnp.swapaxes(a, 0, 1)
        bT = jnp.swapaxes(b, 0, 1)
        cT = jnp.swapaxes(c, 0, 1)
        s0 = jnp.zeros((x.shape[0], Wa.shape[1]), x.dtype)
        _, csT = jax.lax.scan(step, s0, (aT, bT, cT))
        cs = jnp.swapaxes(csT, 0, 1)
        y = jnp.einsum('btn,nd->btd', cs, Wy) + by + d
        return y

    def _L0_ffn_ref(x, ln_gamma, ln_beta, gate_w, w1, w2):
        import jax, jax.numpy as jnp
        import numpy as np
        E = 8
        K = 2
        C = 256
        F = 512
        EPS = 1e-05
        B, T, Cc = x.shape
        xf = x.reshape(-1, Cc)
        mu = jnp.mean(xf, axis=-1, keepdims=True)
        var = jnp.var(xf, axis=-1, keepdims=True)
        rn = (xf - mu) * jax.lax.rsqrt(var + EPS) * ln_gamma + ln_beta
        logits = rn @ gate_w.T
        probs = jax.nn.softmax(logits, axis=-1)
        rw, sel = jax.lax.top_k(probs, K)
        comb = jnp.sum(jax.nn.one_hot(sel, E, dtype=xf.dtype) * rw[..., None], axis=1)
        h = jax.nn.gelu(jnp.einsum('nc,efc->enf', xf, w1), approximate=False)
        y = jnp.einsum('enf,ecf->enc', h, w2)
        out = jnp.einsum('enc,ne->nc', y, comb)
        return out.reshape(B, T, Cc)
    x = L0_attn_x
    xn = _layernorm(x, axis=-1)
    x = x + _L0_attn_ref(xn, L0_attn_Wa, L0_attn_ba, L0_attn_Wb, L0_attn_bb, L0_attn_Wc, L0_attn_bc, L0_attn_Wd, L0_attn_bd, L0_attn_Wy, L0_attn_by) + _L0_ffn_ref(xn, L0_ffn_ln_gamma, L0_ffn_ln_beta, L0_ffn_gate_w, L0_ffn_w1, L0_ffn_w2)
    return x

_drawn_inputs = setup_inputs


def setup_inputs(seed=0):
    import zlib

    import numpy as np

    out = dict(_drawn_inputs(seed))
    spreads = {'L0_attn_ba': (0.0, 0.796),
     'L0_attn_bb': (0.0, 0.1),
     'L0_attn_bc': (0.0, 0.299),
     'L0_attn_bd': (0.0, 0.1),
     'L0_attn_by': (0.0, 0.1)}
    factors = {'L0_ffn_ln_gamma': 39.21, 'L0_ffn_ln_beta': 34.065}
    for name, (base, spread) in spreads.items():
        noise = np.random.default_rng([zlib.crc32(name.encode()), seed]).standard_normal(out[name].shape)
        drawn = base * np.exp(spread * noise) if base else spread * noise
        out[name] = jnp.asarray(drawn.astype(out[name].dtype))
    for name, factor in factors.items():
        out[name] = (out[name] * factor).astype(out[name].dtype)
    return out
```

```python
from contextlib import ExitStack

import concourse.bass as bass
from concourse import mybir

F32 = mybir.dt.float32
F16 = mybir.dt.float16
I32 = mybir.dt.int32
ALU = mybir.AluOpType
ACT = mybir.ActivationFunctionType
AX = mybir.AxisListType

P = 128
BATCH, SEQ, D = 4, 2048, 256
TOKENS = BATCH * SEQ
N = 64
E, F, TOP = 8, 512, 2
KC = D // P
FC = F // P
GROUP = 512
SUB = GROUP // P
GROUPS = TOKENS // GROUP
TT = TOKENS // P
TILE = 256
TSUB = TILE // P
N_TILES = (TOP * TOKENS + E * (TILE - 1)) // TILE
COLS = N_TILES * TSUB
NO_TOKEN = 1 << 20
EPS = 1e-5
X_SCALE, W_SCALE = 8.0, 64.0
SCALE = X_SCALE * W_SCALE
WCHUNK = 2 * KC * F
SC = 16
GATE_SPLIT, ALL_SPLIT = 2, 8
CENTRED, SECOND, CHOSEN, ROUTED = 3, 8, 13, 40
PARTS = ((0, 0), (0, 1), (1, 0))


class Step:

    def __init__(self, turn, offset, unroll=2):
        self.turn, self.offset, self.unroll = turn, offset, unroll
        self.i = turn * unroll + offset
        self.buf = offset % 2
        self.half = turn * (unroll // 2) + offset // 2

    def plus(self, n):
        return Step(self.turn, self.offset + n, self.unroll)


def run_steps(eng, count, stages, unroll=2, peel=0):
    last_lag = max(lag for lag, _ in stages)
    head = -(-max(last_lag, peel) // unroll) * unroll
    turns = (count - head) // unroll

    def straight(g):
        for lag, emit in stages:
            if 0 <= g - lag < count:
                emit(Step(0, g - lag, unroll))

    for g in range(head):
        straight(g)
    with eng.Fori(0, turns) as turn:
        for place in range(unroll):
            for lag, emit in stages:
                emit(Step(turn, head + place - lag, unroll))
    for g in range(head + turns * unroll, count + last_lag):
        straight(g)


def park(eng, mark):
    eng.sem_inc(mark, 1)


class Signal:

    def __init__(self, sem, per=1, depth=2):
        self.sem, self.per, self.depth = sem, per, depth

    def give_credit(self, eng):
        eng.sem_inc(self.sem, self.per * self.depth)

    def done(self, eng, step, k=None):
        eng.wait_ge(self.sem, (step.i + self.depth) * self.per + (self.per if k is None else k))

    def free(self, eng, step, k=None):
        eng.wait_ge(self.sem, step.i * self.per + (self.per if k is None else k))

    def all(self, eng, count):
        eng.wait_ge(self.sem, (count + self.depth) * self.per)


class DmaSignal:

    def __init__(self, sems, per=1, credit=True):
        self.sems, self.per, self.credit = sems, 16 * per, int(credit)

    def give_credit(self, eng):
        if self.credit:
            for sem in self.sems:
                eng.sem_inc(sem, self.per)

    def inc(self, dma, step):
        dma.then_inc(self.sems[step.buf], 16)

    def done(self, eng, step):
        turns = step.half + 1 + self.credit
        if not isinstance(turns, int) or turns > 0:
            eng.wait_ge(self.sems[step.buf], turns * self.per)

    def free(self, eng, step):
        turns = step.half + self.credit
        if not isinstance(turns, int) or turns > 0:
            eng.wait_ge(self.sems[step.buf], turns * self.per)

    def all(self, eng, count):
        for buf, sem in enumerate(self.sems):
            eng.wait_ge(sem, ((count + 1 - buf) // 2 + self.credit) * self.per)


def build(nc, x, wa, wb, wc, wd, wy, cols, rows, gate, gamma_beta, experts, out):
    x_tok = x.rearrange("b (c p) d -> p (b c) d", p=P)
    out_tok = out.rearrange("b (c p) d -> p (b c) d", p=P)
    out_rows = out.rearrange("b t d -> (b t) d")
    xn_dram = nc.dram_tensor("xn_rows", [TOKENS, 2 * D], F16, kind="Internal").ap()
    table_dram = nc.dram_tensor("slot_table", [P * COLS, 2], I32, kind="Internal").ap()
    xn_tok = xn_dram.rearrange("(c p) d -> p c d", p=P)

    with ExitStack() as ctx:
        def sb(name, shape, dt):
            return ctx.enter_context(nc.sbuf_tensor(name, shape, dt))

        def sem(name):
            return ctx.enter_context(nc.semaphore(name))

        def signal(name, per=1, depth=2):
            return Signal(sem(name), per, depth)

        def dma_signal(name, per=1, credit=True):
            return DmaSignal([sem(f"{name}_{b}") for b in range(2)], per, credit)

        xT = sb("xT", [P, 2 * KC * TOKENS], F16)
        xTv = xT[:, :].rearrange("p (h k t) -> p h k t", h=2, k=KC)
        w16 = sb("w16", [P, 2 * E, WCHUNK], F16)
        w16_flat = w16[:, :, :].rearrange("p e w -> p (e w)")
        xin = sb("xin", [P, 2, SUB, D], F32)
        x8 = sb("x8", [P, 2, SUB, D], F32)
        xn16 = sb("xn16", [P, 2, SUB, 2, D], F16)
        wstage = sb("wstage", [P, 2, WCHUNK // 2], F32)
        ident = sb("ident", [P, P], F16)
        before = sb("before", [P, P], F16)
        ones16 = sb("ones16", [P, P], F16)
        onesf = sb("onesf", [P, GROUP], F32)
        small32 = sb("small32", [P, KC, 2 * N + N + D], F32)
        small16 = sb("small16", [P, 2, KC, 2 * N + N + D], F16)
        wy32 = sb("wy32", [N + 1, D], F32)
        bd_row = sb("bd_row", [N + 1, D], F32)
        wy16 = sb("wy16", [N + 1, 2, D], F16)
        gate32 = sb("gate32", [P, KC, E], F32)
        gated = sb("gated", [P, KC, E], F32)
        gate16 = sb("gate16", [P, 2, KC, E], F16)
        gb = sb("gb", [P, 2, KC], F32)
        beta_b = sb("beta_b", [P, KC, P], F32)
        bias8 = sb("bias8", [P, E], F32)
        col = sb("col", [N, 3], F32)
        bb_s = sb("bb_s", [N, 1], F32)
        eps = sb("eps", [P, 1], F32)
        bn = sb("bn", [P, 2, SUB, 6], F32)
        mv = sb("mv", [P, 2, SUB, 2], F32)
        sd = sb("sd", [P, 2, SUB], F32)
        rs = sb("rs", [P, 2, SUB], F32)
        rs8 = sb("rs8", [P, 2, SUB], F32)
        table = sb("table", [P, COLS, 2], I32)
        pair_val = sb("pair_val", [P, TOP * TT, 2], I32)
        pair_row = sb("pair_row", [P, TOP * TT], I32)
        sc_row = sb("sc_row", [P, 2, SC], I32)
        sc_val = sb("sc_val", [P, 2, SC, 2], I32)
        expert_off = sb("expert_off", [1, N_TILES], I32)
        gidx = sb("gidx", [P, 2, TSUB], I32)
        rank = sb("rank", [P, E], F32)
        tile_start = sb("tile_start", [1, N_TILES], F32)
        sidx = sb("sidx", [P, TSUB], I32)
        ac = xn16[:, :, :, :, :].rearrange("p b s h d -> p b (s h d)").bitcast(F32)
        a_sb = [ac[0:N, b, 0:GROUP] for b in range(2)]
        c_sb = [ac[0:N, b, GROUP:2 * GROUP] for b in range(2)]
        oma = sb("oma", [N, GROUP], F32)
        u_sb = sb("u_sb", [N, GROUP], F32)
        state = sb("state", [N, 2, GROUP], F32)
        cs8 = sb("cs8", [N, GROUP], F32)
        cs16 = sb("cs16", [N + 1, 2, 2, GROUP], F16)
        w16_f32, w16_i32 = w16_flat.bitcast(F32), w16_flat.bitcast(I32)
        space = [0]

        def temp(width, whole=None):
            view = w16_f32 if whole is None else whole
            piece = view[:, space[0]:space[0] + width]
            space[0] += width
            return piece

        (r_logit, r_exp, r_one1, r_one2, r_rest, r_tmp, r_tot, r_keep, r_run, r_slot) = (
            temp(TT * E) for _ in range(10))
        chosen16 = temp(TT * E // 2).bitcast(F16)
        r_max1, r_max2, r_exp2, r_rank, r_sum = (temp(TT) for _ in range(5))
        r_pair = temp(TOP * TT)
        r_islot, r_ilow, r_ihigh = (temp(TOP * TT, w16_i32) for _ in range(3))
        r_int, r_int2 = (temp(E, w16_i32) for _ in range(2))
        r_pad, r_end, r_start = (temp(E) for _ in range(3))
        r_te = temp(N_TILES)[0:1, :]
        at = [0]

        def carve(size, dt=F16):
            width = size * (2 if dt == F32 else 1)
            piece = xT[:, at[0]:at[0] + width]
            at[0] += width
            return piece.bitcast(F32) if dt == F32 else piece

        xg = [[carve(2 * D) for _ in range(TSUB)] for _ in range(2)]
        tT = [carve(2 * KC * TILE).rearrange("p (h k t) -> p h k t", h=2, k=KC) for _ in range(2)]
        h32 = [[carve(2 * TILE, F32) for _ in range(2)] for _ in range(2)]
        h16 = [carve(2 * FC * TILE).rearrange("p (h f t) -> p h f t", h=2, f=FC) for _ in range(2)]
        ys = [carve(TSUB * D, F32).rearrange("p (s d) -> p s d", s=TSUB) for _ in range(2)]

        ps = ctx.enter_context(nc.psum_tensor("ps", [P, 8, 512], F32))

        def bank(b):
            return ps[:, b, :]

        def bank16(b):
            return ps[:, b, :].bitcast(F16)

        s_ident, s_const, s_small, s_betab, s_bias8 = (sem(n) for n in (
            "s_ident", "s_const", "s_small", "s_betab", "s_bias8"))
        s_ld = [sem(f"s_ld{j}") for j in range(10)]
        s_prep = sem("s_prep")
        x_in = dma_signal("x_in")
        stats, aggr, root, recip, rscale = (signal(n) for n in ("stats", "aggr", "root", "recip", "rscale"))
        x8_made, hi_made, lo_made = signal("x8_made"), signal("hi_made"), signal("lo_made")
        stored = dma_signal("stored")
        turned = signal("turned", 2)
        moved = signal("moved", 2)
        scored = signal("scored")
        s_route = sem("s_route")
        s_exp = sem("s_exp")
        s_count = sem("s_count")
        s_fill = sem("s_fill")
        picked = signal("picked")
        scattered = dma_signal("scattered", SC, credit=False)
        s_table = sem("s_table")
        s_tab0 = sem("s_tab0")
        w_in = dma_signal("w_in")
        w_hi, w_lo = signal("w_hi"), signal("w_lo")
        projected = signal("projected", 2)
        gates = signal("gates", 2)
        om_made, u_made, s_made, cs_made, cshi, cslo = (signal(n) for n in (
            "om_made", "u_made", "s_made", "cs_made", "cshi", "cslo"))
        summed = signal("summed", 2)
        added = signal("added", 2)
        out_put = dma_signal("out_put")
        s_cs1 = sem("s_cs1")
        gi_made = signal("gi_made")
        gathered = dma_signal("gathered", TSUB, credit=False)
        g_turned, g_moved = signal("g_turned"), signal("g_moved", 2)
        hidden = signal("hidden", 2)
        gelued = signal("gelued", 2)
        hhi, hlo = signal("hhi", 2), signal("hlo", 2)
        y_made, y_out = signal("y_made"), signal("y_out")
        si_made = signal("si_made", 1, 1)
        put_back = dma_signal("put_back", TSUB, credit=False)
        s_mark = sem("s_mark")
        s_clear = sem("s_clear")
        every = [stats, aggr, root, recip, rscale, x8_made, hi_made, lo_made, turned, moved, scored,
                 x_in, stored, picked, scattered, w_in, w_hi, w_lo, projected, gates, om_made, u_made,
                 s_made, cs_made, cshi, cslo, summed, added, out_put, gi_made, gathered, g_turned, g_moved,
                 hidden, gelued, hhi, hlo, y_made, y_out, si_made, put_back]

        block = ctx.enter_context(nc.Block())

        @block.sync
        def _(sp):
            for s in every:
                s.give_credit(sp)

            def load_x(step, first=0):
                x_in.inc(sp.dma_start(xin[:, step.buf, :, :], x_tok[:, bass.ds(step.i * SUB - first, SUB), :]), step)

            def load_x_again(step):
                load_x(step.plus(GROUPS), TT)

            def load_w(step):
                w_in.inc(sp.dma_start(wstage[:, step.buf, :], experts[:, bass.ds(step.i, 1), :]), step)

            load_x(Step(0, 0))
            sp.dma_start(gate32[:, :, :], gate).then_inc(s_ld[0], 16)
            sp.dma_start(gb[:, :, :], gamma_beta).then_inc(s_ld[1], 16)
            load_x(Step(0, 1))
            for j, (w, c0, c1) in enumerate(((wa, 0, N), (wb, N, 2 * N), (wc, 2 * N, 3 * N), (wd, 3 * N, 3 * N + D))):
                sp.dma_start(small32[:, :, c0:c1], w.rearrange("(k p) n -> p k n", p=P)).then_inc(s_ld[2 + j], 16)
            sp.dma_start(wy32[0:N, :], wy).then_inc(s_ld[6], 16)
            sp.dma_start(wy32[N:N + 1, :], rows[0:1, :]).then_inc(s_ld[7], 16)
            sp.dma_start(bd_row[N:N + 1, :], rows[1:2, :]).then_inc(s_ld[8], 16)
            sp.dma_start(col[:, :], cols).then_inc(s_ld[9], 16)

            def store_xn(step):
                lo_made.done(sp, step)
                stored.inc(sp.dma_start(xn_tok[:, bass.ds(step.i * SUB, SUB), :],
                                        xn16[:, step.buf, :, :, :].rearrange("p s h d -> p s (h d)")), step)

            def stage1(step, load, ahead):
                x8_made.done(sp, step)
                load(ahead)
                store_xn(step)

            with sp.Fori(0, GROUPS // 2 - 1) as turn:
                for place in range(2):
                    stage1(Step(turn, place), load_x, Step(turn, place + 2))
            for place in range(2):
                stage1(Step(0, GROUPS - 2 + place), load_x_again, Step(0, place))
            for place in range(2):
                load_w(Step(0, place))

            sp.wait_ge(s_fill, 1)
            sp.dma_start(table_dram.rearrange("(p c) v -> p c v", p=P), table[:, :, :]).then_inc(s_tab0, 16)

            def stage3(step, last=False):
                added.done(sp, step)
                out_put.inc(sp.dma_start(out_tok[:, bass.ds(step.i * SUB, SUB), :], x8[:, step.buf, :, :]), step)
                if not last:
                    load_x_again(step.plus(2))
                    w_lo.done(sp, step)
                    load_w(step.plus(2))

            with sp.Fori(0, GROUPS // 4 - 1) as turn:
                for place in range(4):
                    stage3(Step(turn, place, 4))
            for place in range(4):
                stage3(Step(0, GROUPS - 4 + place, 4), last=place >= 2)
            scattered.all(sp, TOP * TT // SC)
            sp.dma_start(table[:, :, :], table_dram.rearrange("(p c) v -> p c v", p=P)).then_inc(s_table, 16)
            out_put.all(sp, GROUPS)
            put_back.all(sp, N_TILES)

        @block.gpsimd
        def _(pool):
            pool.memset(ident[:, :], 0.0).then_inc(s_ident, 1)
            pool.memset(ones16[:, :], 1.0).then_inc(s_ident, 1)
            pool.wait_ge(s_ident, 2)
            pool.affine_select(out=ident[:, :], in_=ident[:, :], compare_op=ALU.not_equal, fill=1.0, base=0,
                               pattern=[[-1, P]], channel_multiplier=1).then_inc(s_ident, 1)
            pool.affine_select(out=before[:, :], in_=ones16[:, :], compare_op=ALU.is_gt, fill=0.0, base=0,
                               pattern=[[1, P]], channel_multiplier=-1).then_inc(s_const, 1)
            pool.memset(onesf[:, :], 1.0).then_inc(s_const, 1)
            pool.memset(table[:, :, :], 0).then_inc(s_const, 1)
            pool.iota(rank[:, :], [[-1, E]], base=E, channel_multiplier=0,
                      allow_small_or_imprecise_dtypes=True).then_inc(s_const, 1)
            pool.iota(tile_start[0:1, :], [[TILE, N_TILES]], base=0, channel_multiplier=0,
                      allow_small_or_imprecise_dtypes=True).then_inc(s_const, 1)
            pool.iota(pair_val[:, 0:TT, 0], [[P, TT]], base=0, channel_multiplier=1).then_inc(s_const, 1)
            pool.iota(pair_val[:, TT:2 * TT, 0], [[P, TT]], base=0, channel_multiplier=1).then_inc(s_const, 1)
            pool.wait_ge(s_const, 7)
            pool.memset(cs16[N:N + 1, :, :, :], 0.0).then_inc(s_cs1, 1)
            pool.wait_ge(s_cs1, 1)
            pool.memset(cs16[N:N + 1, :, 0, :], X_SCALE).then_inc(s_cs1, 1)
            pool.wait_ge(s_cs1, 2)
            pool.memset(table[:, :, 0], NO_TOKEN).then_inc(s_fill, 1)

            def pick(step):
                scattered.free(pool, step)
                park(pool, s_mark)
                pool.tensor_copy(sc_row[:, step.buf, :], pair_row[:, bass.ds(step.i * SC, SC)])
                pool.tensor_copy(sc_val[:, step.buf, :, :],
                                 pair_val[:, bass.ds(step.i * SC, SC), :]).then_inc(picked.sem, 1)

            def scatter(step):
                picked.done(pool, step)
                park(pool, s_mark)
                for j in range(SC):
                    scattered.inc(pool.indirect_dma_start(
                        table_dram[:, :], bass.IndirectOffsetOnAxis(ap=sc_row[:, step.buf, j:j + 1], axis=0),
                        sc_val[:, step.buf, j, :], None), step)

            pool.wait_ge(s_route, ROUTED)
            pool.wait_ge(s_tab0, 16)
            run_steps(pool, TOP * TT // SC, [(0, pick), (0, scatter)], peel=2)

            pool.wait_ge(s_clear, 1)
            stored.all(pool, GROUPS)
            out_put.all(pool, GROUPS)
            pool.wait_ge(s_table, 16)

            def gather(step):
                gathered.free(pool, step)
                park(pool, s_mark)
                pool.tensor_copy(gidx[:, step.buf, :], table[:, bass.ds(step.i * TSUB, TSUB), 0]).then_inc(gi_made.sem, 1)
                g_turned.free(pool, step)
                gi_made.done(pool, step)
                park(pool, s_mark)
                for s in range(TSUB):
                    gathered.inc(pool.indirect_dma_start(
                        xg[step.buf][s], None, xn_dram[:, :],
                        bass.IndirectOffsetOnAxis(ap=gidx[:, step.buf, s:s + 1], axis=0),
                        bounds_check=TOKENS - 1, oob_is_err=False), step)

            def add_back(step):
                if step.offset > 0:
                    put_back.done(pool, step.plus(-1))
                park(pool, s_mark)
                pool.tensor_copy(sidx[:, :], table[:, bass.ds(step.i * TSUB, TSUB), 0]).then_inc(si_made.sem, 1)
                y_out.done(pool, step)
                si_made.done(pool, step)
                park(pool, s_mark)
                for s in range(TSUB):
                    put_back.inc(pool.indirect_dma_start(
                        out_rows, bass.IndirectOffsetOnAxis(ap=sidx[:, s:s + 1], axis=0),
                        ys[step.buf][:, s, :], None, bounds_check=TOKENS - 1, oob_is_err=False,
                        compute_op=ALU.add), step)

            run_steps(pool, N_TILES, [(0, gather), (4, add_back)], peel=6)

        @block.tensor
        def _(pe):
            pe.wait_ge(s_ident, 3)

            def transposes(step):
                lo_made.done(pe, step)
                for h in range(2):
                    moved.free(pe, step, h + 1)
                    dst = bank16(2 * step.buf + h).rearrange("p (k t) -> p k t", k=KC)
                    for k in range(KC):
                        for s in range(SUB):
                            t = pe.transpose(dst[:, k, s * P:(s + 1) * P], xn16[:, step.buf, s, h, k * P:(k + 1) * P],
                                             ident[:, :])
                    t.then_inc(turned.sem, 1)

            def scores(step):
                moved.done(pe, step)
                park(pe, s_mark)
                for s in range(SUB):
                    n = 0
                    for k in range(KC):
                        for a, b in PARTS:
                            m = pe.matmul(bank(4)[:, bass.ds(step.i * SUB * E + s * E, E)],
                                          xTv[:, a, k, bass.ds(step.i * GROUP + s * P, P)], gate16[:, b, k, :],
                                          start=(n == 0), stop=(n == 2 * KC + 1))
                            n += 1
                m.then_inc(scored.sem, 1)

            pe.wait_ge(s_betab, 1)
            for k in range(KC):
                m = pe.matmul(bank(7)[:, 0:E], beta_b[:, k, :], gate32[:, k, :], start=(k == 0), stop=(k == KC - 1))
            m.then_inc(s_bias8, 1)
            pe.wait_ge(s_small, GATE_SPLIT)
            run_steps(pe, GROUPS, [(0, transposes), (1, scores)])

            pe.wait_ge(s_route, CHOSEN)
            pe.wait_ge(s_const, 7)
            pe.matmul(bank(5), before[:, :], chosen16, start=True, stop=True)
            pe.matmul(bank(6), ones16[:, :], chosen16, start=True, stop=True).then_inc(s_count, 1)
            pe.wait_ge(s_small, ALL_SPLIT)
            pe.wait_ge(s_cs1, 2)

            def project(step):
                toks = bass.ds(step.i * GROUP, GROUP)
                for out_bank, c0, c1 in ((step.buf, 0, 2 * N), (2 + step.buf, 2 * N, 3 * N)):
                    if c0 == 0:
                        u_made.free(pe, step)
                    gates.free(pe, step, 1 if c0 == 0 else 2)
                    park(pe, s_mark)
                    n = 0
                    for k in range(KC):
                        for a, b in PARTS:
                            m = pe.matmul(bank(out_bank)[0:c1 - c0, :], small16[:, b, k, c0:c1], xTv[:, a, k, toks],
                                          start=(n == 0), stop=(n == 2 * KC + 1))
                            n += 1
                    m.then_inc(projected.sem, 1)

            def sums(step):
                cslo.done(pe, step)
                for j in range(2):
                    added.free(pe, step, j + 1)
                    park(pe, s_mark)
                    for s in (2 * j, 2 * j + 1):
                        dst = bank(4 + 2 * step.buf + j)[:, (s % 2) * D:(s % 2 + 1) * D]
                        n = 0
                        for k in range(KC):
                            for a, b in PARTS:
                                pe.matmul(dst, xTv[:, a, k, bass.ds(step.i * GROUP + s * P, P)],
                                          small16[:, b, k, 3 * N:3 * N + D], start=(n == 0), stop=False)
                                n += 1
                        for n, (a, b) in enumerate(PARTS):
                            m = pe.matmul(dst, cs16[:, step.buf, a, s * P:(s + 1) * P], wy16[:, b, :],
                                          start=False, stop=(n == 2))
                    m.then_inc(summed.sem, 1)

            run_steps(pe, GROUPS, [(0, project), (1, sums)], unroll=4)

            gates.all(pe, GROUPS)
            added.all(pe, GROUPS)
            w_lo.all(pe, GROUPS)

            def g_transposes(step):
                gathered.done(pe, step)
                g_moved.free(pe, step)
                dst = bank16(6 + step.buf).rearrange("p (h k t) -> p h k t", h=2, k=KC)
                for s in range(TSUB):
                    for h in range(2):
                        for k in range(KC):
                            t = pe.transpose(dst[:, h, k, s * P:(s + 1) * P],
                                             xg[step.buf][s][:, h * D + k * P:h * D + (k + 1) * P], ident[:, :])
                t.then_inc(g_turned.sem, 1)

            def up(step):
                off = pe.value_load(expert_off[0:1, bass.ds(step.i, 1)], min_val=0, max_val=(E - 1) * WCHUNK)
                g_moved.done(pe, step)
                for q in range(2):
                    gelued.free(pe, step, q + 1)
                    park(pe, s_mark)
                    for f in (2 * q, 2 * q + 1):
                        dst = bank(2 * step.buf + q)[:, (f % 2) * TILE:(f % 2 + 1) * TILE]
                        n = 0
                        for k in range(KC):
                            for a, b in PARTS:
                                m = pe.matmul(dst, w16_flat[:, bass.ds(off + ((b * KC + k) * F + f * P), P)],
                                              tT[step.buf][:, a, k, :], start=(n == 0), stop=(n == 2 * KC + 1))
                                n += 1
                    m.then_inc(hidden.sem, 1)

            def down(step):
                off = pe.value_load(expert_off[0:1, bass.ds(step.i, 1)], min_val=0, max_val=(E - 1) * WCHUNK)
                hlo.done(pe, step)
                y_out.free(pe, step)
                park(pe, s_mark)
                for s in range(TSUB):
                    n = 0
                    for f in range(FC):
                        for b, a in PARTS:
                            m = pe.matmul(bank(4 + step.buf)[:, s * D:(s + 1) * D],
                                          h16[step.buf][:, a, f, s * P:(s + 1) * P],
                                          w16_flat[:, bass.ds(off + (E * WCHUNK + (b * FC + f) * D), D)],
                                          start=(n == 0), stop=(n == 3 * FC - 1))
                            n += 1
                m.then_inc(y_made.sem, 1)

            run_steps(pe, N_TILES, [(0, g_transposes), (1, up), (2, down)])

        @block.scalar
        def _(act):
            def square_root(step):
                aggr.done(act, step)
                act.activation(sd[:, step.buf, :], mv[:, step.buf, :, 1], ACT.Sqrt,
                               bias=eps[:, 0:1]).then_inc(root.sem, 1)

            def high(step):
                x8_made.done(act, step)
                turned.free(act, step)
                stored.free(act, step)
                act.copy(xn16[:, step.buf, :, 0, :], x8[:, step.buf, :, :]).then_inc(hi_made.sem, 1)

            def move(step):
                for h in range(2):
                    turned.done(act, step, h + 1)
                    park(act, s_mark)
                    act.copy(xTv[:, h, :, bass.ds(step.i * GROUP, GROUP)],
                             bank16(2 * step.buf + h).rearrange("p (k t) -> p k t", k=KC)).then_inc(moved.sem, 1)

            act.wait_ge(s_prep, 1)
            run_steps(act, GROUPS, [(0, square_root), (2, move), (0, high)])

            act.wait_ge(s_route, CENTRED)
            act.activation(r_exp, r_logit, ACT.Exp).then_inc(s_exp, 1)
            act.wait_ge(s_route, SECOND)
            act.activation(r_exp2, r_max2, ACT.Exp).then_inc(s_exp, 1)

            stored.all(act, GROUPS)
            act.wait_ge(s_small, ALL_SPLIT)
            act.wait_ge(s_route, ROUTED)
            act.wait_ge(s_count, 1)

            def gate(step):
                projected.done(act, step, 1)
                s_made.free(act, step)
                act.activation(a_sb[step.buf], bank(step.buf)[0:N, :], ACT.Sigmoid, bias=col[:, 0:1],
                               scale=1.0 / SCALE).then_inc(gates.sem, 1)
                projected.done(act, step, 2)
                cs_made.free(act, step)
                act.activation(c_sb[step.buf], bank(2 + step.buf)[0:N, :], ACT.Tanh, bias=col[:, 2:3],
                               scale=1.0 / SCALE).then_inc(gates.sem, 1)

            def weight_high(step):
                w_in.done(act, step)
                park(act, s_mark)
                act.mul(w16[:, bass.ds(step.i, 1), 0:WCHUNK // 2], wstage[:, bass.ds(step.buf, 1), :],
                        W_SCALE).then_inc(w_hi.sem, 1)

            run_steps(act, GROUPS, [(0, gate), (0, weight_high)], unroll=4)

            act.wait_ge(s_table, 16)
            act.wait_ge(s_clear, 1)
            weights = table[:, :, :].bitcast(F32)

            def gelu(step):
                for q in range(2):
                    hidden.done(act, step, q + 1)
                    hlo.free(act, step, q + 1)
                    act.activation(h32[step.buf][q], bank(2 * step.buf + q), ACT.Gelu,
                                   scale=1.0 / SCALE).then_inc(gelued.sem, 1)

            def weigh(step):
                y_made.done(act, step)
                put_back.free(act, step)
                park(act, s_mark)
                for s in range(TSUB):
                    y = act.mul(ys[step.buf][:, s, :], bank(4 + step.buf)[:, s * D:(s + 1) * D],
                                weights[:, bass.ds(step.i * TSUB + s, 1), 1])
                y.then_inc(y_out.sem, 1)

            run_steps(act, N_TILES, [(1, gelu), (2, weigh)], peel=4)

        @block.vector
        def _(dve):
            dve.memset(eps[:, :], EPS).then_inc(s_prep, 1)
            dve.wait_ge(s_ld[0], 16)
            dve.wait_ge(s_ld[1], 16)
            split_count = [0]

            def split(src, high_part, low_part, scale):
                dve.tensor_scalar(high_part, src, scale, None, ALU.mult).then_inc(s_small, 1)
                split_count[0] += 1
                dve.wait_ge(s_small, split_count[0])
                dve.scalar_tensor_tensor(out=low_part, in0=src, scalar=scale, in1=high_part, op0=ALU.mult,
                                         op1=ALU.subtract).then_inc(s_small, 1)
                split_count[0] += 1

            for k in range(KC):
                dve.tensor_scalar(gated[:, k, :], gate32[:, k, :], gb[:, 0, k:k + 1], None, ALU.mult).then_inc(s_prep, 1)
            dve.tensor_copy(beta_b[:, :, :], gb[:, 1, :].unsqueeze(2).to_broadcast([P, KC, P])).then_inc(s_betab, 1)
            dve.wait_ge(s_prep, 1 + KC)
            split(gated[:, :, :], gate16[:, 0, :, :], gate16[:, 1, :, :], W_SCALE)
            assert split_count[0] == GATE_SPLIT
            for s in s_ld[2:]:
                dve.wait_ge(s, 16)
            for c0, c1 in ((0, 3 * N), (3 * N, 3 * N + D)):
                split(small32[:, :, c0:c1], small16[:, 0, :, c0:c1], small16[:, 1, :, c0:c1], W_SCALE)
            dve.tensor_tensor(wy32[N:N + 1, :], wy32[N:N + 1, :], bd_row[N:N + 1, :], ALU.add).then_inc(s_prep, 1)
            dve.tensor_scalar(bb_s[:, :], col[:, 1:2], SCALE, None, ALU.mult).then_inc(s_prep, 1)
            dve.wait_ge(s_prep, 3 + KC)
            split(wy32[:, :], wy16[:, 0, :], wy16[:, 1, :], W_SCALE)
            assert split_count[0] == ALL_SPLIT
            dve.wait_ge(s_bias8, 1)
            dve.tensor_copy(bias8[:, :], bank(7)[:, 0:E]).then_inc(s_prep, 1)

            def statistics(step):
                x_in.done(dve, step)
                for s in range(SUB):
                    b = dve.bn_stats(bn[:, step.buf, s, :], xin[:, step.buf, s, :])
                b.then_inc(stats.sem, 1)
                stats.done(dve, step)
                park(dve, s_mark)
                for s in range(SUB):
                    b = dve.bn_aggr(mv[:, step.buf, s, :], bn[:, step.buf, s, :])
                b.then_inc(aggr.sem, 1)

            def low(step):
                hi_made.done(dve, step)
                dve.tensor_tensor(xn16[:, step.buf, :, 1, :], x8[:, step.buf, :, :], xn16[:, step.buf, :, 0, :],
                                  ALU.subtract).then_inc(lo_made.sem, 1)

            def normalize(step):
                root.done(dve, step)
                dve.reciprocal(rs[:, step.buf, :], sd[:, step.buf, :]).then_inc(recip.sem, 1)
                recip.done(dve, step)
                dve.tensor_scalar(rs8[:, step.buf, :], rs[:, step.buf, :], X_SCALE, None, ALU.mult)\
                   .then_inc(rscale.sem, 1)
                rscale.done(dve, step)
                for s in range(SUB):
                    n = dve.tensor_scalar(x8[:, step.buf, s, :], xin[:, step.buf, s, :], mv[:, step.buf, s, 0:1],
                                          rs8[:, step.buf, s:s + 1], ALU.subtract, ALU.mult)
                    if s == SUB - 1:
                        n.then_inc(x8_made.sem, 1)

            run_steps(dve, GROUPS, [(0, statistics), (1, low), (0, normalize)])

            steps = [0]

            def then(instruction, name=None):
                steps[0] += 1
                instruction.then_inc(s_route, 1)
                dve.wait_ge(s_route, steps[0])
                if name is not None:
                    assert steps[0] == name, (steps[0], name)

            def by_e(ap):
                return ap.unsqueeze(2).to_broadcast([P, TT, E])

            dve.wait_ge(s_const, 7)
            dve.wait_ge(s_prep, 4 + KC)
            scored.all(dve, GROUPS)
            logit = r_logit.rearrange("p (t e) -> p t e", e=E)
            ranks = rank[:, :].unsqueeze(1).to_broadcast([P, TT, E])
            then(dve.scalar_tensor_tensor(out=logit, in0=bank(4).rearrange("p (t e) -> p t e", e=E), scalar=1.0 / SCALE,
                                          in1=bias8[:, :].unsqueeze(1).to_broadcast([P, TT, E]), op0=ALU.mult,
                                          op1=ALU.add))
            then(dve.tensor_reduce(r_max1, logit, AX.X, ALU.max))
            then(dve.tensor_tensor(logit, logit, by_e(r_max1), ALU.subtract), CENTRED)

            def choose(src, top, one_hot, scratch):
                v = scratch.rearrange("p (t e) -> p t e", e=E)
                if top is None:
                    then(dve.scalar_tensor_tensor(out=v, in0=src, scalar=0.0, in1=ranks, op0=ALU.is_equal, op1=ALU.mult))
                else:
                    then(dve.tensor_tensor(v, src, by_e(top), ALU.is_equal))
                    then(dve.tensor_tensor(v, v, ranks, ALU.mult))
                then(dve.tensor_reduce(r_rank, v, AX.X, ALU.max))
                then(dve.tensor_tensor(one_hot.rearrange("p (t e) -> p t e", e=E), v, by_e(r_rank), ALU.is_equal))

            choose(logit, None, r_one1, r_tmp)
            rest = r_rest.rearrange("p (t e) -> p t e", e=E)
            then(dve.scalar_tensor_tensor(out=r_rest, in0=r_one1, scalar=-1e30, in1=r_logit, op0=ALU.mult, op1=ALU.add))
            then(dve.tensor_reduce(r_max2, rest, AX.X, ALU.max), SECOND)
            choose(rest, r_max2, r_one2, r_tmp)
            then(dve.tensor_tensor(chosen16, r_one1, r_one2, ALU.add), CHOSEN)
            dve.wait_ge(s_count, 1)
            totals = r_tot.rearrange("p (e t) -> p e t", e=E)
            then(dve.tensor_copy(totals, bank(6).rearrange("p (t e) -> p e t", e=E)))
            then(dve.tensor_copy(r_keep, onesf[:, :]))
            then(dve.memset(r_keep.rearrange("p (e t) -> p e t", e=E)[:, :, 0:1], 0.0))
            then(dve.tensor_tensor_scan(r_run, r_keep, r_tot, 0.0, ALU.mult, ALU.add))
            run = r_run.rearrange("p (e t) -> p e t", e=E)
            then(dve.tensor_scalar(r_int, run[:, :, TT - 1], float(TILE - 1), None, ALU.add))
            then(dve.tensor_scalar(r_int2, r_int, 8, None, ALU.logical_shift_right))
            then(dve.tensor_scalar(r_pad, r_int2, float(TILE), None, ALU.mult))
            then(dve.tensor_tensor_scan(r_end, onesf[:, 0:E], r_pad, 0.0, ALU.mult, ALU.add))
            then(dve.tensor_tensor(r_start, r_end, r_pad, ALU.subtract))
            then(dve.tensor_tensor(r_run, r_run, r_tot, ALU.subtract))
            slot = r_slot.rearrange("p (t e) -> p t e", e=E)
            then(dve.tensor_tensor(slot, run.rearrange("p e t -> p t e"),
                                   r_start.unsqueeze(1).to_broadcast([P, TT, E]), ALU.add))
            then(dve.tensor_tensor(r_slot, bank(5), r_slot, ALU.add))
            for j, one in enumerate((r_one1, r_one2)):
                then(dve.tensor_tensor(r_tmp, one, r_slot, ALU.mult))
                then(dve.tensor_reduce(r_pair[:, j * TT:(j + 1) * TT], r_tmp.rearrange("p (t e) -> p t e", e=E),
                                       AX.X, ALU.add))
            then(dve.tensor_copy(r_islot, r_pair))
            then(dve.tensor_scalar(r_ilow, r_islot, P - 1, None, ALU.bitwise_and))
            then(dve.tensor_scalar(r_ihigh, r_islot, 7, None, ALU.logical_shift_right))
            then(dve.scalar_tensor_tensor(out=pair_row[:, :], in0=r_ilow, scalar=float(COLS), in1=r_ihigh,
                                          op0=ALU.mult, op1=ALU.add))
            dve.wait_ge(s_exp, 2)
            then(dve.tensor_reduce(r_sum, r_exp.rearrange("p (t e) -> p t e", e=E), AX.X, ALU.add))
            then(dve.reciprocal(r_rank, r_sum))
            pair_weight = pair_val[:, :, :].bitcast(F32)
            then(dve.tensor_scalar(pair_weight[:, 0:TT, 1], r_rank, 1.0 / SCALE, None, ALU.mult))
            then(dve.scalar_tensor_tensor(out=pair_weight[:, TT:2 * TT, 1], in0=r_exp2, scalar=1.0 / SCALE,
                                          in1=r_rank, op0=ALU.mult, op1=ALU.mult))
            cmp = r_tmp[0:1, 0:N_TILES * (E - 1)].rearrange("p (j e) -> p j e", e=E - 1)
            then(dve.tensor_tensor(cmp, tile_start[0:1, :].unsqueeze(2).to_broadcast([1, N_TILES, E - 1]),
                                   r_end[0:1, 0:E - 1].unsqueeze(1).to_broadcast([1, N_TILES, E - 1]), ALU.is_ge))
            then(dve.tensor_reduce(r_te, cmp, AX.X, ALU.add))
            then(dve.tensor_scalar(expert_off[0:1, :], r_te, float(WCHUNK), None, ALU.mult), ROUTED)

            def recur(step):
                gates.done(dve, step, 1)
                dve.tensor_scalar(oma[:, :], a_sb[step.buf], -1.0 / SCALE, 1.0 / SCALE, ALU.mult, ALU.add)\
                   .then_inc(om_made.sem, 1)
                om_made.done(dve, step)
                dve.scalar_tensor_tensor(out=u_sb[:, :], in0=bank(step.buf)[N:2 * N, :], scalar=bb_s[:, 0:1],
                                         in1=oma[:, :], op0=ALU.add, op1=ALU.mult).then_inc(u_made.sem, 1)
                u_made.done(dve, step)
                initial = 0.0 if step.offset % (SEQ // GROUP) == 0 else state[:, 1 - step.buf, GROUP - 1:GROUP]
                dve.tensor_tensor_scan(state[:, step.buf, :], a_sb[step.buf], u_sb[:, :], initial, ALU.mult,
                                       ALU.add).then_inc(s_made.sem, 1)
                s_made.done(dve, step)
                gates.done(dve, step, 2)
                dve.scalar_tensor_tensor(out=cs8[:, :], in0=c_sb[step.buf], scalar=X_SCALE, in1=state[:, step.buf, :],
                                         op0=ALU.mult, op1=ALU.mult).then_inc(cs_made.sem, 1)
                cs_made.done(dve, step)
                summed.free(dve, step)
                dve.tensor_copy(cs16[0:N, step.buf, 0, :], cs8[:, :]).then_inc(cshi.sem, 1)
                cshi.done(dve, step)
                dve.tensor_tensor(cs16[0:N, step.buf, 1, :], cs8[:, :], cs16[0:N, step.buf, 0, :], ALU.subtract)\
                   .then_inc(cslo.sem, 1)

            def weight_low(step):
                w_hi.done(dve, step)
                dve.scalar_tensor_tensor(out=w16[:, bass.ds(step.i, 1), WCHUNK // 2:WCHUNK],
                                         in0=wstage[:, bass.ds(step.buf, 1), :], scalar=W_SCALE,
                                         in1=w16[:, bass.ds(step.i, 1), 0:WCHUNK // 2], op0=ALU.mult,
                                         op1=ALU.subtract).then_inc(w_lo.sem, 1)

            def add_x(step):
                x_in.done(dve, step.plus(GROUPS))
                out_put.free(dve, step)
                for j in range(2):
                    summed.done(dve, step, j + 1)
                    s = 2 * j
                    dve.scalar_tensor_tensor(out=x8[:, step.buf, s:s + 2, :].rearrange("p s d -> p (s d)"),
                                             in0=bank(4 + 2 * step.buf + j), scalar=1.0 / SCALE,
                                             in1=xin[:, step.buf, s:s + 2, :].rearrange("p s d -> p (s d)"),
                                             op0=ALU.mult, op1=ALU.add).then_inc(added.sem, 1)

            run_steps(dve, GROUPS, [(0, recur), (0, weight_low), (1, add_x)], unroll=4)

            gathers = [xg[b][s] for b in range(2) for s in range(TSUB)]
            for g in gathers:
                m = dve.memset(g, 0.0)
            m.then_inc(s_clear, 1)

            def g_move(step):
                g_turned.done(dve, step)
                hidden.free(dve, step)
                for h in range(2):
                    dve.tensor_copy(tT[step.buf][:, h, :, :].rearrange("p k t -> p (k t)"),
                                    bank16(6 + step.buf)[:, h * KC * TILE:(h + 1) * KC * TILE])\
                       .then_inc(g_moved.sem, 1)

            def h_split(step):
                for q in range(2):
                    gelued.done(dve, step, q + 1)
                    if q == 0:
                        y_made.free(dve, step)
                    high_part = h16[step.buf][:, 0, 2 * q:2 * q + 2, :].rearrange("p f t -> p (f t)")
                    low_part = h16[step.buf][:, 1, 2 * q:2 * q + 2, :].rearrange("p f t -> p (f t)")
                    dve.tensor_scalar(high_part, h32[step.buf][q], X_SCALE, None, ALU.mult).then_inc(hhi.sem, 1)
                    hhi.done(dve, step, q + 1)
                    dve.scalar_tensor_tensor(out=low_part, in0=h32[step.buf][q], scalar=X_SCALE, in1=high_part,
                                             op0=ALU.mult, op1=ALU.subtract).then_inc(hlo.sem, 1)

            run_steps(dve, N_TILES, [(0, g_move), (1, h_split)])


def kernel(**inputs):
    import numpy as np
    import concourse.bacc as bacc
    from concourse.bass_utils import run_bass_kernel_spmd

    def arr(name):
        return np.asarray(inputs[name])

    w1 = arr("L0_ffn_w1").reshape(E, F, KC, P).transpose(3, 0, 2, 1).reshape(P, E, KC * F)
    w2 = arr("L0_ffn_w2").reshape(E, D, FC, P).transpose(3, 0, 2, 1).reshape(P, E, FC * D)
    laid_out = {
        "x": arr("L0_attn_x"), "wa": arr("L0_attn_Wa"), "wb": arr("L0_attn_Wb"), "wc": arr("L0_attn_Wc"),
        "wd": arr("L0_attn_Wd"), "wy": arr("L0_attn_Wy"),
        "cols": np.stack([arr("L0_attn_ba"), arr("L0_attn_bb"), arr("L0_attn_bc")], axis=1),
        "rows": np.stack([arr("L0_attn_by"), arr("L0_attn_bd")]),
        "gate": arr("L0_ffn_gate_w").reshape(E, KC, P).transpose(2, 1, 0),
        "gamma_beta": np.stack([arr("L0_ffn_ln_gamma"), arr("L0_ffn_ln_beta")]).reshape(2, KC, P).transpose(2, 0, 1),
        "experts": np.concatenate([w1, w2], axis=1),
    }
    nc = bacc.Bacc("TRN2", target_bir_lowering=False, num_devices=1)
    arrays, args = {}, []
    for name, a in laid_out.items():
        a = np.ascontiguousarray(a)
        arrays[f"in_{name}"] = a
        args.append(nc.dram_tensor(f"in_{name}", a.shape, mybir.dt.from_np(a.dtype), kind="ExternalInput").ap())
    args.append(nc.dram_tensor("out_0", (BATCH, SEQ, D), F32, kind="ExternalOutput").ap())
    build(nc, *args)
    return run_bass_kernel_spmd(nc, [arrays], core_ids=[0]).results[0]["out_0"]
```

```python
from contextlib import ExitStack
from functools import partial
from itertools import chain, cycle

import concourse.bass as bass
from concourse import mybir

F32 = mybir.dt.float32
F16 = mybir.dt.float16
I32 = mybir.dt.int32
ALU = mybir.AluOpType
ACT = mybir.ActivationFunctionType
AX = mybir.AxisListType

P = 128
BATCH, SEQ, D = 4, 2048, 256
TOKENS = BATCH * SEQ
N = 64
E, F, TOP = 8, 512, 2
KC = D // P
FC = F // P
GROUP = 512
SUB = GROUP // P
GROUPS = TOKENS // GROUP
PAIRS_OF_GROUPS = GROUPS // 2
SEQ_GROUPS = SEQ // GROUP
BATCHES = PAIRS_OF_GROUPS
BT = 2 * SUB
TT = TOKENS // P
PAIRS = TOP * BT
TILE = 256
TSUB = TILE // P
N_TILES = (TOP * TOKENS + E * (TILE - 1)) // TILE
LIST_ROWS = (E - 1) * TOKENS + N_TILES * TILE
FILL = LIST_ROWS // P
FIRST_TILES = 6
NO_TOKEN = 1 << 20
EPS = 1e-5
NEWTON = 17
MAGIC = 0x5F3759DF
X_SCALE, W_SCALE = 8.0, 64.0
SCALE = X_SCALE * W_SCALE
WCHUNK = 2 * KC * F
GATE_SPLIT, ALL_SPLIT, BIASED, PLANNED = 2, 14, 15, 13
LOGITS, CENTRED, SECOND, CHOSEN, COUNTS_READ, PLACED, ROUTED = 1, 4, 9, 14, 16, 25, 30
PARTS = ((0, 0), (0, 1), (1, 0))


END = object()


class Step:

    def __init__(self, turn, offset, unroll=2):
        self.turn, self.offset, self.unroll = turn, offset, unroll
        self.i = turn * unroll + offset
        self.buf = offset % 2
        self.half = turn * (unroll // 2) + offset // 2

    def pair(self):
        return Step(self.turn, self.offset // 2, self.unroll // 2)

    def plus(self, n):
        return Step(self.turn, self.offset + n, self.unroll)


def run_steps(eng, count, stages, unroll=2, peel=0, emit_step=None):
    last_lag = max(lag for lag, _ in stages)
    head = -(-max(last_lag, peel) // unroll) * unroll
    turns = (count - head) // unroll

    def one_step(work):
        if emit_step is not None:
            emit_step(work)
        else:
            for emit, step in work:
                emit(step)

    def straight(g):
        one_step([(emit, Step(0, g - lag, unroll)) for lag, emit in stages if 0 <= g - lag < count])

    for g in range(head):
        straight(g)
    with eng.Fori(0, turns) as turn:
        for place in range(unroll):
            one_step([(emit, Step(turn, head + place - lag, unroll)) for lag, emit in stages])
    for g in range(head + turns * unroll, count + last_lag):
        straight(g)


def park(eng, mark):
    eng.sem_inc(mark, 1)


class Signal:

    def __init__(self, sem, per=1, depth=2):
        self.sem, self.per, self.depth = sem, per, depth

    def give_credit(self, eng):
        if self.depth:
            eng.sem_inc(self.sem, self.per * self.depth)

    def done(self, eng, step, k=None, back=0):
        assert back <= self.depth
        eng.wait_ge(self.sem, (step.i + (self.depth - back)) * self.per + (self.per if k is None else k))

    def all(self, eng, count):
        eng.wait_ge(self.sem, (count + self.depth) * self.per)


class DmaSignal:

    def __init__(self, sems, per=1, credit=True):
        self.sems, self.per, self.credit = sems, 16 * per, int(credit)

    def give_credit(self, eng):
        if self.credit:
            for sem in self.sems:
                eng.sem_inc(sem, self.per)

    def inc(self, dma, step):
        dma.then_inc(self.sems[step.buf], 16)

    def done(self, eng, step):
        turns = step.half + 1 + self.credit
        if not isinstance(turns, int) or turns > 0:
            eng.wait_ge(self.sems[step.buf], turns * self.per)

    def free(self, eng, step):
        turns = step.half + self.credit
        if not isinstance(turns, int) or turns > 0:
            eng.wait_ge(self.sems[step.buf], turns * self.per)

    def all(self, eng, count):
        for buf, sem in enumerate(self.sems):
            eng.wait_ge(sem, ((count + 1 - buf) // 2 + self.credit) * self.per)


def build(nc, x, wa, wb, wc, wd, wy, cols, rows, gate, gamma_beta, experts, out):
    x_tok = x.rearrange("(w b) (c p) d -> p w (b c) d", w=2, p=P)
    out_tok = out.rearrange("(w b) (c p) d -> p w (b c) d", w=2, p=P)
    out_rows = out.rearrange("b t d -> (b t) d")
    xn_dram = nc.dram_tensor("xn_rows", [TOKENS, 2 * D], F16, kind="Internal").ap()
    list_dram = nc.dram_tensor("expert_lists", [LIST_ROWS, 2], I32, kind="Internal").ap()
    xn_tok = xn_dram.rearrange("(w c p) d -> p w c d", w=2, p=P)

    with ExitStack() as ctx:
        def sb(name, shape, dt):
            return ctx.enter_context(nc.sbuf_tensor(name, shape, dt))

        def sem(name):
            return ctx.enter_context(nc.semaphore(name))

        def signal(name, per=1, depth=2):
            return Signal(sem(name), per, depth)

        def dma_signal(name, per=1, credit=True):
            return DmaSignal([sem(f"{name}_{b}") for b in range(2)], per, credit)

        w16 = sb("w16", [P, 2 * E, WCHUNK], F16)
        w16_flat = w16[:, :, :].rearrange("p e w -> p (e w)")
        ident = sb("ident", [P, P], F16)
        before = sb("before", [P, P], F16)
        ones16 = sb("ones16", [P, P], F16)
        keep = sb("keep", [P, E, BT], F32)
        rank = sb("rank", [P, E], F32)
        list_start = sb("list_start", [P, E], F32)
        one_row = sb("one_row", [1, E], F32)
        tile_no = sb("tile_no", [1, N_TILES], F32)
        fill = sb("fill", [P, FILL, 2], I32)
        abc32 = sb("abc32", [P, KC, 3, N], F32)
        abc16 = sb("abc16", [P, 2, KC, 3, 3 * N], F16)
        wd32 = sb("wd32", [P, KC, D], F32)
        wd16 = sb("wd16", [P, 2, KC, D], F16)
        wy32 = sb("wy32", [2 * N, D], F32)
        wy16 = sb("wy16", [2 * N, 2, 2, D], F16)
        by_row, bd_row, bias_row = (sb(n, [1, D], F32) for n in ("by_row", "bd_row", "bias_row"))
        bias16 = sb("bias16", [1, 2, D], F16)
        eights = sb("eights", [1, P], F16)
        gate32 = sb("gate32", [P, KC, E], F32)
        gated = sb("gated", [P, KC, E], F32)
        gate16 = sb("gate16", [P, 2, KC, E], F16)
        gb = sb("gb", [P, 2, KC], F32)
        beta_b = sb("beta_b", [P, KC, P], F32)
        bias8 = sb("bias8", [P, E], F32)
        col = sb("col", [2 * N, 3], F32)
        ba_half, bb_s, half, minus_one = (sb(n, [2 * N, 1], F32) for n in ("ba_half", "bb_s", "half", "minus_one"))
        carry = sb("carry", [2 * N, PAIRS_OF_GROUPS], F32)
        xin = sb("xin", [P, 2, 2 * SUB, D], F32)
        x_res = sb("x_res", [P, 2, SUB, D], F32)
        x8 = sb("x8", [P, 2, SUB, D], F32)
        out_sb = sb("out_sb", [P, 2, SUB, D], F32)
        xn16 = sb("xn16", [P, 2, SUB, 2, D], F16)
        xT = sb("xT", [P, 4, 2, KC, GROUP], F16)
        w_stage = sb("w_stage", [P, 2, WCHUNK // 2], F32)
        w_scale, zero = sb("w_scale", [P, 1], F32), sb("zero", [P, 1], F32)
        bn = sb("bn", [P, 2 * SUB, 6], F32)
        mv = sb("mv", [P, 2 * SUB, 2], F32)
        ve, nh, nq, ny, nz = (sb(n, [P, 2, 2 * SUB], F32) for n in ("ve", "nh", "nq", "ny", "nz"))
        root = sb("root", [P, 2 * SUB], F32)
        router_norm = sb("router_norm", [P, TT], F32)
        rs8 = sb("rs8", [P, 2, 2 * SUB], F32)
        nmr8 = sb("nmr8", [P, 2, 2 * SUB], F32)
        tanh_a = sb("tanh_a", [2 * N, GROUP], F32)
        a_sb = sb("a_sb", [2 * N, 2, GROUP], F32)
        m_sb = sb("m_sb", [2 * N, 2, GROUP], F32)
        c_sb = sb("c_sb", [2 * N, 2, GROUP], F32)
        u_sb = sb("u_sb", [2 * N, GROUP], F32)
        initial = sb("initial", [2 * N, 1], F32)
        state = sb("state", [2 * N, 2, GROUP], F32)
        cs8 = sb("cs8", [2 * N, GROUP], F32)
        cs16 = sb("cs16", [2 * N, 2, 2, GROUP], F16)
        (r_logit, r_exp, r_one1, r_one2, r_rest, r_tmp, r_tot, r_run, r_slot) = (
            sb(n, [P, BT * E], F32)[:, :] for n in ("r_logit", "r_exp", "r_one1", "r_one2", "r_rest", "r_tmp",
                                                     "r_tot", "r_run", "r_slot"))
        chosen16 = sb("chosen16", [P, BT * E], F16)
        r_max1, r_max2, r_exp2, r_rank, r_sum = (
            sb(n, [P, BT], F32)[:, :] for n in ("r_max1", "r_max2", "r_exp2", "r_rank", "r_sum"))
        next_row = sb("next_row", [P, E], F32)
        pair_val = sb("pair_val", [P, 2, PAIRS, 2], I32)
        r_row = sb("r_row", [P, PAIRS], F32)
        pair_row = sb("pair_row", [P, 2, PAIRS], I32)
        r_int, r_int2 = (sb(n, [1, E], I32)[:, :] for n in ("r_int", "r_int2"))
        r_cnt, r_tiles, r_end = (sb(n, [1, E], F32)[:, :] for n in ("r_cnt", "r_tiles", "r_end"))
        r_cmp = sb("r_cmp", [1, N_TILES, E - 1], F32)
        r_te, r_first, r_off = (sb(n, [1, N_TILES], F32) for n in ("r_te", "r_first", "r_off"))
        expert_off = sb("expert_off", [1, N_TILES], I32)
        tile_row = sb("tile_row", [1, N_TILES], I32)
        tokens = sb("tokens", [P, TOP, 2, SUB], I32)
        table = sb("table", [P, N_TILES * TSUB, 2], I32)
        gidx = sb("gidx", [P, 2, TSUB], I32)
        sidx = sb("sidx", [P, TSUB], I32)
        xg = [[sb(f"xg{b}{s}", [P, 2 * D], F16)[:, :] for s in range(TSUB)] for b in range(2)]
        xT_flat = xT[:, :, :, :, :].rearrange("p b h k t -> p (b h k t)")
        xin_flat = xin[:, :, :, :].rearrange("p b s d -> p (b s d)")
        split_size, h32_size, tT_size, ys_size = 2 * FC * TILE, 4 * TILE, 2 * KC * TILE // 2, TSUB * D
        h16 = [xT_flat[:, b * split_size:(b + 1) * split_size].rearrange("p (h f t) -> p h f t", h=2, f=FC)
               for b in range(2)]
        h32 = [[xT_flat[:, 2 * split_size + (2 * b + q) * h32_size:2 * split_size + (2 * b + q + 1) * h32_size]
                .bitcast(F32) for q in range(2)] for b in range(2)]
        tT = [xin_flat[:, b * tT_size:(b + 1) * tT_size].bitcast(F16).rearrange("p (h k t) -> p h k t", h=2, k=KC)
              for b in range(2)]
        ys = [xin_flat[:, 2 * tT_size + b * ys_size:2 * tT_size + (b + 1) * ys_size]
              .rearrange("p (s d) -> p s d", s=TSUB) for b in range(2)]

        ps = ctx.enter_context(nc.psum_tensor("ps", [P, 8, 512], F32))
        B_TURN, B_A, B_B, B_C, B_ROUTE, B_SUM = 0, 2, 3, 4, 5, 6
        SCORE_COL, COUNT_COL = 0, BT * E

        def bank(b):
            return ps[:, b, :]

        def bank16(b):
            return ps[:, b, :].bitcast(F16)

        s_ident, s_const, s_small, s_betab, s_fill, s_filled, s_prep = (sem(n) for n in (
            "s_ident", "s_const", "s_small", "s_betab", "s_fill", "s_filled", "s_prep"))
        s_bias8 = sem("s_bias8")
        s_ld = [sem(f"s_ld{j}") for j in range(12)]
        x_in, x_again = dma_signal("x_in", 2), dma_signal("x_again")
        stats, newton = signal("stats", 2, 0), signal("newton", NEWTON, 0)
        x8_made, hi_made = signal("x8_made", depth=3), signal("hi_made")
        lo_made = signal("lo_made")
        stored = dma_signal("stored")
        turned = signal("turned", 2)
        moved = signal("moved", 2)
        scored = signal("scored")
        projected = signal("projected", 3)
        gates = signal("gates", 4)
        u_made, init_made, s_made, cs_made, cshi, cslo = (
            signal(n) for n in ("u_made", "init_made", "s_made", "cs_made", "cshi", "cslo"))
        summed = signal("summed", 2, 4)
        added = signal("added", 2)
        out_put = dma_signal("out_put")
        w1_in = dma_signal("w1_in", credit=False)
        w1_scaled, w1_hi, w1_lo = signal("w1_scaled"), signal("w1_hi"), signal("w1_lo")
        w2_in = dma_signal("w_in")
        w2_hi, w2_lo = signal("w2_hi"), signal("w2_lo")
        route = signal("route", ROUTED, 0)
        exped = signal("exped", 2, 0)
        counted = signal("counted", 1, 0)
        s_scatter = sem("s_scatter")
        spread = signal("spread", 1, 2)
        s_plan = sem("s_plan")
        fetched = dma_signal("fetched")
        gi_made = signal("gi_made")
        gathered = dma_signal("gathered", TSUB, credit=False)
        g_turned, g_moved = signal("g_turned"), signal("g_moved", 2)
        hidden = signal("hidden", 2)
        gelued = signal("gelued", 2)
        hhi, hlo = signal("hhi", 2), signal("hlo", 2)
        y_made, y_out = signal("y_made"), signal("y_out")
        si_made = signal("si_made")
        put_back = dma_signal("put_back", TSUB, credit=False)
        s_mark = sem("s_mark")
        s_clear = sem("s_clear")
        every = [fetched, x_in, x_again, x8_made, hi_made, lo_made, stored, turned, moved, scored, projected, gates,
                 u_made, init_made, s_made, cs_made, cshi, cslo, summed, added, out_put, w1_scaled, w1_hi, w1_lo, w2_in, w2_hi, w2_lo, spread, gi_made,
                 g_turned, g_moved, hidden, gelued, hhi, hlo, y_made, y_out, si_made]

        block = ctx.enter_context(nc.Block())

        @block.sync
        def _(sp):
            for s in every:
                s.give_credit(sp)

            def half_rows(tok, step):
                return tok[:, step.buf, bass.ds(step.half * SUB, SUB), :]

            def load_x(step):
                if step.offset % 2 == 0:
                    x8_made.done(sp, step, back=3)
                    park(sp, s_mark)
                    for w in range(2):
                        x_in.inc(sp.dma_start(xin[:, step.pair().buf, w * SUB:(w + 1) * SUB, :],
                                              half_rows(x_tok, step.plus(w))), step.pair())

            def load_w2(step):
                w1_lo.all(sp, E)
                w2_lo.done(sp, step, back=2)
                park(sp, s_mark)
                w2_in.inc(sp.dma_start(w_stage[:, step.buf:step.buf + 1, :], experts[:, bass.ds(step.i + E, 1), :]), step)

            def load_first_w2(step):
                if isinstance(step.i, int) and step.i >= GROUPS - 2:
                    load_w2(Step(0, step.i - (GROUPS - 2)))

            def store_xn(step):
                lo_made.done(sp, step)
                park(sp, s_mark)
                stored.inc(sp.dma_start(half_rows(xn_tok, step),
                                        xn16[:, step.buf, :, :, :].rearrange("p s h d -> p s (h d)")), step)

            def load_x_again(step):
                added.done(sp, step, back=2)
                park(sp, s_mark)
                x_again.inc(sp.dma_start(x_res[:, step.buf, :, :], half_rows(x_tok, step)), step)

            def store_out(step):
                added.done(sp, step)
                park(sp, s_mark)
                out_put.inc(sp.dma_start(half_rows(out_tok, step), out_sb[:, step.buf, :, :]), step)

            load_x(Step(0, 0, 4))
            sp.dma_start(gate32[:, :, :], gate).then_inc(s_ld[0], 16)
            sp.dma_start(gb[:, :, :], gamma_beta).then_inc(s_ld[1], 16)
            for w, source in enumerate((wa, wb, wc)):
                sp.dma_start(abc32[:, :, w, :], source.rearrange("(k p) n -> p k n", p=P)).then_inc(s_ld[2 + w], 16)
            sp.wait_ge(s_fill, 2)
            sp.dma_start(list_dram.rearrange("(p c) v -> p c v", p=P), fill[:, :, :]).then_inc(s_filled, 16)

            def load_x_once(step):
                if step.offset > 0 or not isinstance(step.i, int):
                    load_x(step)

            run_steps(sp, GROUPS, [(0, load_x_once), (3, store_xn), (7, store_out), (5, load_x_again),
                                   (5, load_first_w2)], unroll=4)
            run_steps(sp, E - 2, [(0, lambda step: load_w2(step.plus(2)))])

            sp.wait_ge(s_plan, PLANNED)
            spread.all(sp, BATCHES)

            def fetch(step):
                fetched.free(sp, step)
                row = sp.value_load(tile_row[0:1, bass.ds(step.i, 1)], min_val=0, max_val=LIST_ROWS - TILE)
                fetched.inc(sp.dma_start(table[:, bass.ds(step.i * TSUB, TSUB), :],
                                         list_dram[bass.ds(row, TILE), :].rearrange("(p s) v -> p s v", s=TSUB)), step)

            run_steps(sp, N_TILES, [(0, fetch)])
            out_put.all(sp, GROUPS)
            put_back.all(sp, N_TILES)

        @block.gpsimd
        def _(pool):
            pool.memset(ident[:, :], 0.0).then_inc(s_ident, 1)
            pool.memset(ones16[:, :], 1.0).then_inc(s_ident, 1)
            pool.wait_ge(s_ident, 2)
            pool.affine_select(out=ident[:, :], in_=ident[:, :], compare_op=ALU.not_equal, fill=1.0, base=0,
                               pattern=[[-1, P]], channel_multiplier=1).then_inc(s_ident, 1)
            pool.affine_select(out=before[:, :], in_=ones16[:, :], compare_op=ALU.is_gt, fill=0.0, base=0,
                               pattern=[[1, P]], channel_multiplier=-1).then_inc(s_const, 1)
            pool.memset(keep[:, :, :], 1.0).then_inc(s_const, 1)
            pool.iota(rank[:, :], [[-1, E]], base=E, channel_multiplier=0,
                      allow_small_or_imprecise_dtypes=True).then_inc(s_const, 1)
            pool.iota(tile_no[0:1, :], [[1, N_TILES]], base=0, channel_multiplier=0,
                      allow_small_or_imprecise_dtypes=True).then_inc(s_const, 1)
            for k in range(TOP):
                pool.iota(tokens[:, k, :, :], [[TOKENS // 2, 2], [P, SUB]], base=-GROUP, channel_multiplier=1)\
                    .then_inc(s_const, 1)
            pool.iota(list_start[:, :], [[TOKENS, E]], base=0, channel_multiplier=0,
                      allow_small_or_imprecise_dtypes=True).then_inc(s_const, 1)
            pool.iota(next_row[:, :], [[TOKENS, E]], base=0, channel_multiplier=0,
                      allow_small_or_imprecise_dtypes=True).then_inc(s_const, 1)
            pool.memset(w_scale[:, :], W_SCALE).then_inc(s_const, 1)
            pool.memset(zero[:, :], 0.0).then_inc(s_const, 1)
            pool.memset(fill[:, :, :], 0).then_inc(s_fill, 1)
            pool.wait_ge(s_const, 10)
            pool.wait_ge(s_fill, 1)
            pool.memset(keep[:, :, 0:1], 0.0).then_inc(s_const, 1)
            pool.memset(fill[:, :, 0], NO_TOKEN).then_inc(s_fill, 1)
            pool.wait_ge(s_fill, 2)
            for b in range(2):
                for s in range(TSUB):
                    pool.memset(xg[b][s], 0.0).then_inc(s_clear, 1)
            pool.wait_ge(s_clear, 2 * TSUB)

            def load_w1(step):
                w1_lo.done(pool, step, back=2)
                park(pool, s_mark)
                w1_in.inc(pool.dma_start(w_stage[:, step.buf, :], experts[:, bass.ds(step.i, 1), :]), step)

            def split_w1(step):
                scaled = w_stage[:, step.buf:step.buf + 1, :]
                high_part = w16[:, bass.ds(step.i, 1), 0:WCHUNK // 2]
                w1_in.done(pool, step)
                park(pool, s_mark)
                pool.tensor_tensor(scaled, scaled, w_scale[:, :].unsqueeze(2).to_broadcast([P, 1, WCHUNK // 2]), ALU.mult)\
                    .then_inc(w1_scaled.sem, 1)
                w1_scaled.done(pool, step)
                park(pool, s_mark)
                pool.tensor_tensor(high_part, scaled, zero[:, :].unsqueeze(2).to_broadcast([P, 1, WCHUNK // 2]), ALU.add)\
                    .then_inc(w1_hi.sem, 1)
                w1_hi.done(pool, step)
                park(pool, s_mark)
                pool.tensor_tensor(w16[:, bass.ds(step.i, 1), WCHUNK // 2:WCHUNK], scaled, high_part, ALU.subtract)\
                    .then_inc(w1_lo.sem, 1)

            run_steps(pool, E, [(0, load_w1), (1, split_w1)])
            w1_lo.all(pool, E)

            pool.wait_ge(s_filled, 16)
            with pool.Fori(0, BATCHES // 2) as turn:
                for buf in range(2):
                    batch = Step(turn, buf)
                    route.done(pool, batch)
                    park(pool, s_mark)
                    for j in range(PAIRS):
                        pool.indirect_dma_start(list_dram[:, :],
                                                bass.IndirectOffsetOnAxis(ap=pair_row[:, buf, j:j + 1], axis=0),
                                                pair_val[:, buf, j, :], None).then_inc(s_scatter, 16)
                    pool.wait_ge(s_scatter, (batch.i + 1) * (16 * PAIRS))
                    pool.sem_inc(spread.sem, 1)

            stored.all(pool, GROUPS)

            def gather(step):
                gathered.free(pool, step)
                fetched.done(pool, step)
                park(pool, s_mark)
                pool.tensor_copy(gidx[:, step.buf, :], table[:, bass.ds(step.i * TSUB, TSUB), 0]).then_inc(gi_made.sem, 1)
                g_turned.done(pool, step, back=2)
                gi_made.done(pool, step)
                park(pool, s_mark)
                for s in range(TSUB):
                    gathered.inc(pool.indirect_dma_start(
                        xg[step.buf][s], None, xn_dram[:, :],
                        bass.IndirectOffsetOnAxis(ap=gidx[:, step.buf, s:s + 1], axis=0),
                        bounds_check=TOKENS - 1, oob_is_err=False), step)

            def add_back(step):
                if step.offset > 0:
                    put_back.done(pool, step.plus(-1))
                else:
                    out_put.all(pool, GROUPS)
                park(pool, s_mark)
                pool.tensor_copy(sidx[:, :], table[:, bass.ds(step.i * TSUB, TSUB), 0]).then_inc(si_made.sem, 1)
                y_out.done(pool, step)
                si_made.done(pool, step)
                park(pool, s_mark)
                for s in range(TSUB):
                    put_back.inc(pool.indirect_dma_start(
                        out_rows, bass.IndirectOffsetOnAxis(ap=sidx[:, s:s + 1], axis=0),
                        ys[step.buf][:, s, :], None, bounds_check=TOKENS - 1, oob_is_err=False,
                        compute_op=ALU.add), step)

            run_steps(pool, N_TILES, [(0, gather), (4, add_back)], peel=FIRST_TILES)

        @block.tensor
        def _(pe):
            pe.wait_ge(s_ident, 3)

            def transposes(step):
                lo_made.done(pe, step)
                for h in range(2):
                    moved.done(pe, step, h + 1, back=1)
                    dst = bank16(B_TURN + h).rearrange("p (k t) -> p k t", k=KC)
                    for k in range(KC):
                        for s in range(SUB):
                            t = pe.transpose(dst[:, k, s * P:(s + 1) * P], xn16[:, step.buf, s, h, k * P:(k + 1) * P],
                                             ident[:, :])
                    t.then_inc(turned.sem, 1)

            def scores(step):
                if step.offset > 1 or not isinstance(step.i, int):
                    route.done(pe, step.pair().plus(-1), COUNTS_READ if step.offset % 2 else LOGITS)
                elif step.offset == 0:
                    pe.wait_ge(s_small, GATE_SPLIT)
                    pe.wait_ge(s_prep, BIASED)
                col0 = SCORE_COL + step.buf * (SUB * E)
                for s in range(SUB):
                    n = 0
                    for k in range(KC):
                        for a, b in PARTS:
                            m = pe.matmul(bank(B_ROUTE)[:, col0 + s * E:col0 + (s + 1) * E],
                                          xT[:, step.offset % 4, a, k, s * P:(s + 1) * P], gate16[:, b, k, :],
                                          start=(n == 0), stop=(n == 2 * KC + 1))
                            n += 1
                m.then_inc(scored.sem, 1)

            def project(step):
                moved.done(pe, step)
                if step.offset == 0 and isinstance(step.i, int):
                    pe.wait_ge(s_small, ALL_SPLIT)
                w = step.buf
                for j, out_bank in enumerate((B_A, B_B, B_C)):
                    if w == 0:
                        if j == 1:
                            u_made.done(pe, step.pair(), back=1)
                        else:
                            gates.done(pe, step.pair(), (1, None, 4)[j], back=1)
                    n = 0
                    for k in range(KC):
                        for a, b in PARTS:
                            m = pe.matmul(bank(out_bank), abc16[:, b, k, j, (1 - w) * N:(3 - w) * N],
                                          xT[:, step.offset % 4, a, k, :], start=(w == 0 and n == 0),
                                          stop=(w == 1 and n == 2 * KC + 1))
                            n += 1
                    m.then_inc(projected.sem, 1)

            def sums(step):
                cslo.done(pe, step.pair())
                for j in range(2):
                    added.done(pe, step, j + 1, back=1)
                    for s in (2 * j, 2 * j + 1):
                        dst = bank(B_SUM + j)[:, (s % 2) * D:(s % 2 + 1) * D]
                        n = 0
                        for k in range(KC):
                            for a, b in PARTS:
                                pe.matmul(dst, xT[:, step.offset % 4, a, k, s * P:(s + 1) * P], wd16[:, b, k, :],
                                          start=(n == 0), stop=False)
                                n += 1
                        for a, b in PARTS:
                            pe.matmul(dst, cs16[:, step.pair().buf, a, s * P:(s + 1) * P], wy16[:, step.buf, b, :],
                                      start=False, stop=False)
                        for b in range(2):
                            m = pe.matmul(dst, eights[:, :], bias16[:, b, :], start=False, stop=(b == 1))
                    m.then_inc(summed.sem, 1)

            def counts(step):
                if step.offset % 2:
                    route.done(pe, step.pair(), CHOSEN)
                    for j, matrix in enumerate((before, ones16)):
                        m = pe.matmul(bank(B_ROUTE)[:, COUNT_COL + j * BT * E:COUNT_COL + (j + 1) * BT * E], matrix[:, :],
                                      chosen16[:, :], start=True, stop=True)
                    m.then_inc(counted.sem, 1)

            pe.wait_ge(s_betab, 1)
            for k in range(KC):
                m = pe.matmul(bank(B_ROUTE)[:, 0:E], beta_b[:, k, :], gate32[:, k, :], start=(k == 0), stop=(k == KC - 1))
            m.then_inc(s_bias8, 1)
            pe.wait_ge(s_const, 11)
            run_steps(pe, GROUPS, [(5, counts), (3, project), (2, transposes), (5, sums), (3, scores)], unroll=4)

            added.all(pe, GROUPS)
            w1_lo.all(pe, E)
            w2_lo.all(pe, E)
            pe.wait_ge(s_plan, PLANNED)

            def g_transposes(step):
                gathered.done(pe, step)
                g_moved.done(pe, step, back=2)
                dst = bank16(6 + step.buf).rearrange("p (h k t) -> p h k t", h=2, k=KC)
                for s in range(TSUB):
                    for h in range(2):
                        for k in range(KC):
                            t = pe.transpose(dst[:, h, k, s * P:(s + 1) * P],
                                             xg[step.buf][s][:, h * D + k * P:h * D + (k + 1) * P], ident[:, :])
                t.then_inc(g_turned.sem, 1)

            def up(step):
                off = pe.value_load(expert_off[0:1, bass.ds(step.i, 1)], min_val=0, max_val=(E - 1) * WCHUNK)
                g_moved.done(pe, step)
                for q in range(2):
                    gelued.done(pe, step, q + 1, back=2)
                    park(pe, s_mark)
                    for f in (2 * q, 2 * q + 1):
                        dst = bank(2 * step.buf + q)[:, (f % 2) * TILE:(f % 2 + 1) * TILE]
                        n = 0
                        for k in range(KC):
                            for a, b in PARTS:
                                m = pe.matmul(dst, w16_flat[:, bass.ds(off + ((b * KC + k) * F + f * P), P)],
                                              tT[step.buf][:, a, k, :], start=(n == 0), stop=(n == 2 * KC + 1))
                                n += 1
                    m.then_inc(hidden.sem, 1)

            def down(step):
                off = pe.value_load(expert_off[0:1, bass.ds(step.i, 1)], min_val=0, max_val=(E - 1) * WCHUNK)
                hlo.done(pe, step)
                y_out.done(pe, step, back=2)
                park(pe, s_mark)
                for s in range(TSUB):
                    n = 0
                    for f in range(FC):
                        for b, a in PARTS:
                            m = pe.matmul(bank(4 + step.buf)[:, s * D:(s + 1) * D],
                                          h16[step.buf][:, a, f, s * P:(s + 1) * P],
                                          w16_flat[:, bass.ds(off + (E * WCHUNK + (b * FC + f) * D), D)],
                                          start=(n == 0), stop=(n == 3 * FC - 1))
                            n += 1
                m.then_inc(y_made.sem, 1)

            run_steps(pe, N_TILES, [(0, g_transposes), (1, up), (2, down)])

        @block.scalar
        def _(act):
            act.dma_start(wd32[:, :, :], wd.rearrange("(k p) n -> p k n", p=P)).then_inc(s_ld[5], 16)
            for w in range(2):
                act.dma_start(wy32[w * N:(w + 1) * N, :], wy).then_inc(s_ld[6 + w], 16)
                act.dma_start(col[w * N:(w + 1) * N, :], cols).then_inc(s_ld[8 + w], 16)
            act.dma_start(by_row[:, :], rows[0:1, :]).then_inc(s_ld[10], 16)
            act.dma_start(bd_row[:, :], rows[1:2, :]).then_inc(s_ld[11], 16)

            def x_times_8(step):
                newton.done(act, step.pair())
                lo_made.done(act, step, back=2)
                for s in range(SUB):
                    c = (step.offset % 2) * SUB + s
                    a = act.activation(x8[:, step.buf, s, :], xin[:, step.pair().buf, c, :], ACT.Identity,
                                       bias=nmr8[:, step.pair().buf, c:c + 1], scale=rs8[:, step.pair().buf, c:c + 1])
                a.then_inc(x8_made.sem, 1)

            def high(step):
                x8_made.done(act, step)
                turned.done(act, step, back=2)
                stored.free(act, step)
                act.copy(xn16[:, step.buf, :, 0, :], x8[:, step.buf, :, :]).then_inc(hi_made.sem, 1)

            def move(step):
                summed.done(act, step, back=4)
                for h in range(2):
                    turned.done(act, step, h + 1)
                    act.copy(xT[:, step.offset % 4, h, :, :],
                             bank16(B_TURN + h).rearrange("p (k t) -> p k t", k=KC)).then_inc(moved.sem, 1)

            def gate(step):
                if step.offset % 2 == 0:
                    return
                pair = step.pair()
                if step.offset == 1 and isinstance(step.i, int):
                    act.wait_ge(s_prep, BIASED)
                projected.done(act, step, 1)
                act.activation(tanh_a[:, :], bank(B_A), ACT.Tanh, bias=ba_half[:, 0:1],
                               scale=0.5 / SCALE).then_inc(gates.sem, 1)
                s_made.done(act, pair, back=2)
                cs_made.done(act, pair, back=2)
                gates.done(act, pair, 1)
                act.activation(a_sb[:, pair.buf, :], tanh_a[:, :], ACT.Identity, bias=half[:, 0:1],
                               scale=0.5).then_inc(gates.sem, 1)
                act.activation(m_sb[:, pair.buf, :], tanh_a[:, :], ACT.Identity, bias=minus_one[:, 0:1],
                               scale=1.0).then_inc(gates.sem, 1)
                projected.done(act, step, 3)
                act.activation(c_sb[:, pair.buf, :], bank(B_C), ACT.Tanh, bias=col[:, 2:3],
                               scale=1.0 / SCALE).then_inc(gates.sem, 1)

            def w2_high(step):
                w2_in.done(act, step)
                park(act, s_mark)
                act.mul(w16[:, bass.ds(step.i + E, 1), 0:WCHUNK // 2], w_stage[:, step.buf:step.buf + 1, :],
                        W_SCALE).then_inc(w2_hi.sem, 1)

            def exponentials(step):
                if step.offset % 2:
                    route.done(act, step.pair(), CENTRED)
                    act.activation(r_exp, r_logit, ACT.Exp).then_inc(exped.sem, 1)
                    route.done(act, step.pair(), SECOND)
                    act.activation(r_exp2, r_max2, ACT.Exp).then_inc(exped.sem, 1)

            def normalize_odd(step):
                if step.offset % 2:
                    x_times_8(step)
                    high(step)

            def normalize_even(step):
                if step.offset % 2 == 0:
                    x_times_8(step)
                    high(step)

            run_steps(act, GROUPS, [(5, exponentials), (1, normalize_odd), (3, gate), (2, move), (1, normalize_even)], unroll=4)
            run_steps(act, E, [(0, w2_high)])

            weights = table[:, :, :].bitcast(F32)

            def gelu(step):
                for q in range(2):
                    hidden.done(act, step, q + 1)
                    hlo.done(act, step, q + 1, back=2)
                    act.activation(h32[step.buf][q], bank(2 * step.buf + q), ACT.Gelu,
                                   scale=1.0 / SCALE).then_inc(gelued.sem, 1)

            def weigh(step):
                y_made.done(act, step)
                put_back.free(act, step)
                fetched.done(act, step)
                park(act, s_mark)
                for s in range(TSUB):
                    y = act.mul(ys[step.buf][:, s, :], bank(4 + step.buf)[:, s * D:(s + 1) * D],
                                weights[:, bass.ds(step.i * TSUB + s, 1), 1])
                y.then_inc(y_out.sem, 1)

            run_steps(act, N_TILES, [(1, gelu), (2, weigh)], peel=4)

        @block.vector
        def _(dve):
            dve.memset(half[:, :], 0.5).then_inc(s_prep, 1)
            dve.memset(minus_one[:, :], -1.0).then_inc(s_prep, 1)
            dve.memset(eights[:, :], X_SCALE).then_inc(s_prep, 1)
            dve.memset(state[:, 1, GROUP - 1:GROUP], 0.0).then_inc(s_prep, 1)
            dve.memset(carry[:, :], 1.0).then_inc(s_prep, 1)
            dve.memset(abc16[:, :, :, :, :], 0.0).then_inc(s_prep, 1)
            dve.memset(wy16[:, :, :, :], 0.0).then_inc(s_prep, 1)
            dve.memset(one_row[:, :], 1.0).then_inc(s_prep, 1)
            dve.wait_ge(s_prep, 8)
            dve.memset(carry[:, ::SEQ_GROUPS], 0.0).then_inc(s_prep, 1)
            split_count = [0]

            def split(src, high_part, low_part, scale):
                dve.tensor_scalar(high_part, src, scale, None, ALU.mult).then_inc(s_small, 1)
                split_count[0] += 1
                yield partial(dve.wait_ge, s_small, split_count[0])
                dve.scalar_tensor_tensor(out=low_part, in0=src, scalar=scale, in1=high_part, op0=ALU.mult,
                                         op1=ALU.subtract).then_inc(s_small, 1)
                split_count[0] += 1

            def prepare(step):
                if step.offset != 0 or not isinstance(step.i, int):
                    return
                dve.wait_ge(s_ld[0], 16)
                dve.wait_ge(s_ld[1], 16)
                for k in range(KC):
                    dve.tensor_scalar(gated[:, k, :], gate32[:, k, :], gb[:, 0, k:k + 1], None, ALU.mult).then_inc(s_prep, 1)
                    yield
                dve.tensor_copy(beta_b[:, :, :], gb[:, 1, :].unsqueeze(2).to_broadcast([P, KC, P])).then_inc(s_betab, 1)
                dve.wait_ge(s_prep, 9 + KC)
                yield from split(gated[:, :, :], gate16[:, 0, :, :], gate16[:, 1, :, :], W_SCALE)
                assert split_count[0] == GATE_SPLIT
                for s in s_ld[2:]:
                    dve.wait_ge(s, 16)
                for k in range(KC):
                    yield from split(abc32[:, k, :, :], abc16[:, 0, k, :, N:2 * N], abc16[:, 1, k, :, N:2 * N], W_SCALE)
                yield from split(wd32[:, :, :], wd16[:, 0, :, :], wd16[:, 1, :, :], W_SCALE)
                for w in range(2):
                    rows_w = slice(w * N, (w + 1) * N)
                    yield from split(wy32[rows_w, :], wy16[rows_w, w, 0, :], wy16[rows_w, w, 1, :], W_SCALE)
                dve.tensor_tensor(bias_row[:, :], by_row[:, :], bd_row[:, :], ALU.add).then_inc(s_prep, 1)
                yield
                dve.tensor_scalar(bb_s[:, :], col[:, 1:2], SCALE, None, ALU.mult).then_inc(s_prep, 1)
                yield
                dve.tensor_scalar(ba_half[:, :], col[:, 0:1], 0.5, None, ALU.mult).then_inc(s_prep, 1)
                yield
                dve.wait_ge(s_prep, 12 + KC)
                yield from split(bias_row[:, :], bias16[:, 0, :], bias16[:, 1, :], W_SCALE)
                assert split_count[0] == ALL_SPLIT
                dve.wait_ge(s_bias8, 1)
                dve.tensor_copy(bias8[:, :], bank(B_ROUTE)[:, 0:E]).then_inc(s_prep, 1)
                yield
                assert 13 + KC == BIASED
                dve.wait_ge(s_const, 11)
                yield partial(dve.wait_ge, s_prep, BIASED)

            def take_turns(work):
                odd = any(emit is reciprocal_root and step.offset & 1 for emit, step in work)
                live = {name: chain(*(emit(step) for emit, step in work if track[emit] == name)) for name in "NRT"}
                waits = dict.fromkeys(live)
                for name in cycle("NTNR" if odd else "NTRT"):
                    if name in live:
                        if waits[name] is not None:
                            waits[name]()
                        waits[name] = next(live[name], END)
                        if waits[name] is END:
                            del live[name]
                    if not live:
                        return

            def statistics(step):
                if step.offset % 2 == 0:
                    x_in.done(dve, step.pair())
                first = (step.offset % 2) * SUB
                for s in range(SUB):
                    b = dve.bn_stats(bn[:, first + s, :], xin[:, step.pair().buf, first + s, :])
                    if s == SUB - 1:
                        b.then_inc(stats.sem, 1)
                    yield
                stats.done(dve, step, 1)
                park(dve, s_mark)
                for s in range(SUB):
                    b = dve.bn_aggr(mv[:, first + s, :], bn[:, first + s, :])
                b.then_inc(stats.sem, 1)
                yield

            def reciprocal_root(step):
                if step.offset % 2 == 0:
                    return
                pair = step.pair()
                stats.done(dve, step, 2)
                count = [0]

                def then(instruction):
                    count[0] += 1
                    instruction.then_inc(newton.sem, 1)
                    return partial(newton.done, dve, pair, count[0])

                yield then(dve.tensor_scalar(ve[:, 0, :], mv[:, :, 1], EPS, None, ALU.add))
                yield then(dve.scalar_tensor_tensor(out=ve[:, 1, :], in0=ve[:, 0, :], scalar=EPS, in1=mv[:, :, 1], op0=ALU.mult,
                                              op1=ALU.add))
                yield then(dve.tensor_scalar(nh[:, :, :].bitcast(I32), ve[:, :, :].bitcast(I32), 1, None,
                                       ALU.logical_shift_right))
                yield then(dve.tensor_scalar(ny[:, :, :].bitcast(I32), nh[:, :, :].bitcast(I32), -1.0, float(MAGIC), ALU.mult,
                                       ALU.add))
                y, z = ny, nz
                for _ in range(3):
                    yield then(dve.scalar_tensor_tensor(out=nq[:, :, :], in0=y[:, :, :], scalar=-0.5, in1=y[:, :, :],
                                                  op0=ALU.mult, op1=ALU.mult))
                    yield then(dve.tensor_tensor(nq[:, :, :], nq[:, :, :], ve[:, :, :], ALU.mult))
                    yield then(dve.scalar_tensor_tensor(out=z[:, :, :], in0=nq[:, :, :], scalar=1.5, in1=y[:, :, :],
                                                  op0=ALU.add, op1=ALU.mult))
                    y, z = z, y
                yield then(dve.tensor_scalar(rs8[:, pair.buf, :], y[:, 0, :], X_SCALE, None, ALU.mult))
                yield then(dve.scalar_tensor_tensor(out=nmr8[:, pair.buf, :], in0=mv[:, :, 0], scalar=-1.0,
                                              in1=rs8[:, pair.buf, :], op0=ALU.mult, op1=ALU.mult))
                yield then(dve.tensor_tensor(root[:, :], ve[:, 0, :], y[:, 0, :], ALU.mult))
                yield then(dve.tensor_tensor(router_norm[:, bass.ds(pair.i * (2 * SUB), 2 * SUB)], root[:, :], y[:, 1, :], ALU.mult))
                assert count[0] == NEWTON

            def low(step):
                hi_made.done(dve, step)
                dve.tensor_tensor(xn16[:, step.buf, :, 1, :], x8[:, step.buf, :, :], xn16[:, step.buf, :, 0, :],
                                  ALU.subtract).then_inc(lo_made.sem, 1)
                yield

            def recur(step):
                if step.offset % 2 == 0:
                    return
                group, step = step, step.pair()
                gates.done(dve, step, 3)
                projected.done(dve, group, 2)
                park(dve, s_mark)
                dve.scalar_tensor_tensor(out=u_sb[:, :], in0=bank(B_B), scalar=bb_s[:, 0:1],
                                         in1=m_sb[:, step.buf, :], op0=ALU.add, op1=ALU.mult).then_inc(u_made.sem, 1)
                yield
                dve.tensor_tensor(initial[:, :], state[:, 1 - step.buf, GROUP - 1:GROUP], carry[:, bass.ds(step.i, 1)],
                                  ALU.mult).then_inc(init_made.sem, 1)
                yield
                u_made.done(dve, step)
                init_made.done(dve, step)
                dve.tensor_tensor_scan(state[:, step.buf, :], a_sb[:, step.buf, :], u_sb[:, :], initial[:, 0:1], ALU.mult,
                                       ALU.add).then_inc(s_made.sem, 1)
                yield
                s_made.done(dve, step)
                gates.done(dve, step, 4)
                dve.scalar_tensor_tensor(out=cs8[:, :], in0=c_sb[:, step.buf, :], scalar=-0.5 * X_SCALE / SCALE,
                                         in1=state[:, step.buf, :], op0=ALU.mult, op1=ALU.mult).then_inc(cs_made.sem, 1)
                yield
                cs_made.done(dve, step)
                summed.done(dve, group, back=4)
                dve.tensor_copy(cs16[:, step.buf, 0, :], cs8[:, :]).then_inc(cshi.sem, 1)
                yield
                cshi.done(dve, step)
                dve.tensor_tensor(cs16[:, step.buf, 1, :], cs8[:, :], cs16[:, step.buf, 0, :], ALU.subtract)\
                   .then_inc(cslo.sem, 1)
                yield

            def w2_low(step):
                w2_hi.done(dve, step)
                dve.scalar_tensor_tensor(out=w16[:, bass.ds(step.i + E, 1), WCHUNK // 2:WCHUNK],
                                         in0=w_stage[:, step.buf:step.buf + 1, :], scalar=W_SCALE,
                                         in1=w16[:, bass.ds(step.i + E, 1), 0:WCHUNK // 2], op0=ALU.mult,
                                         op1=ALU.subtract).then_inc(w2_lo.sem, 1)

            def add_x(step):
                x_again.done(dve, step)
                out_put.free(dve, step)
                for j in range(2):
                    summed.done(dve, step, j + 1)
                    s = 2 * j
                    dve.scalar_tensor_tensor(out=out_sb[:, step.buf, s:s + 2, :].rearrange("p s d -> p (s d)"),
                                             in0=bank(B_SUM + j), scalar=1.0 / SCALE,
                                             in1=x_res[:, step.buf, s:s + 2, :].rearrange("p s d -> p (s d)"),
                                             op0=ALU.mult, op1=ALU.add).then_inc(added.sem, 1)
                    yield

            steps = [0]

            def by_e(ap):
                return ap.unsqueeze(2).to_broadcast([P, BT, E])

            def to_e(ap):
                return ap.unsqueeze(1).to_broadcast([P, BT, E])

            def te(ap):
                return ap.rearrange("p (t e) -> p t e", e=E)

            def counter(batch):
                def then(instruction, name=None):
                    steps[0] += 1
                    instruction.then_inc(route.sem, 1)
                    if name is not None:
                        assert steps[0] == name, (steps[0], name)
                    return partial(route.done, dve, batch, steps[0])
                return then

            def centre(step):
                if step.offset % 2 == 0:
                    return
                steps[0] = 0
                then = counter(step.pair())
                scored.done(dve, step)
                logit = te(r_logit)
                products = bank(B_ROUTE)[:, SCORE_COL:SCORE_COL + BT * E]
                norm = router_norm[:, bass.ds(step.pair().i * BT, BT)]
                yield then(dve.scalar_tensor_tensor(out=logit, in0=te(products), scalar=1.0 / SCALE,
                                              in1=by_e(norm), op0=ALU.mult, op1=ALU.mult), LOGITS)
                yield then(dve.tensor_tensor(logit, logit, to_e(bias8[:, :]), ALU.add))
                yield then(dve.tensor_reduce(r_max1, logit, AX.X, ALU.max))
                yield then(dve.tensor_tensor(logit, logit, by_e(r_max1), ALU.subtract), CENTRED)

            def pick(step):
                if step.offset % 2 == 0:
                    return
                steps[0] = CENTRED
                then = counter(step.pair())
                logit, rest = te(r_logit), te(r_rest)

                def choose(src, top, one_hot):
                    v = te(r_tmp)
                    if top is None:
                        yield then(dve.scalar_tensor_tensor(out=v, in0=src, scalar=0.0, in1=to_e(rank[:, :]),
                                                      op0=ALU.is_equal, op1=ALU.mult))
                    else:
                        yield then(dve.tensor_tensor(v, src, by_e(top), ALU.is_equal))
                        yield then(dve.tensor_tensor(v, v, to_e(rank[:, :]), ALU.mult))
                    yield then(dve.tensor_reduce(r_rank, v, AX.X, ALU.max))
                    yield then(dve.tensor_tensor(te(one_hot), v, by_e(r_rank), ALU.is_equal))

                yield from choose(logit, None, r_one1)
                yield then(dve.scalar_tensor_tensor(out=r_rest, in0=r_one1, scalar=-1e30, in1=r_logit, op0=ALU.mult,
                                              op1=ALU.add))
                yield then(dve.tensor_reduce(r_max2, rest, AX.X, ALU.max), SECOND)
                yield from choose(rest, r_max2, r_one2)
                yield then(dve.tensor_tensor(chosen16[:, :], r_one1, r_one2, ALU.add), CHOSEN)

            def place_pairs(step):
                if step.offset % 2 == 0:
                    return
                steps[0] = CHOSEN
                then = counter(step.pair())
                counted.done(dve, step.pair())
                run = r_run.rearrange("p (e t) -> p e t", e=E)
                yield then(dve.tensor_copy(r_tot.rearrange("p (e t) -> p e t", e=E),
                                     bank(B_ROUTE)[:, COUNT_COL + BT * E:COUNT_COL + 2 * BT * E].rearrange("p (t e) -> p e t", e=E)))
                yield then(dve.tensor_tensor(te(r_slot), te(bank(B_ROUTE)[:, COUNT_COL:COUNT_COL + BT * E]),
                                             to_e(next_row[:, :]), ALU.add), COUNTS_READ)
                yield then(dve.tensor_tensor_scan(r_run, keep[:, :, :].rearrange("p e t -> p (e t)"), r_tot, 0.0, ALU.mult,
                                                  ALU.add))
                yield then(dve.tensor_tensor(r_tot, r_run, r_tot, ALU.subtract))
                yield then(dve.tensor_tensor(te(r_slot), te(r_slot), r_tot.rearrange("p (e t) -> p t e", e=E), ALU.add))
                yield then(dve.tensor_tensor(next_row[:, :], next_row[:, :], run[:, :, BT - 1], ALU.add))
                buf = step.pair().buf
                for j, one in enumerate((r_one1, r_one2)):
                    yield then(dve.tensor_tensor(r_tmp, one, r_slot, ALU.mult))
                    yield then(dve.tensor_reduce(r_row[:, j * BT:(j + 1) * BT], te(r_tmp), AX.X, ALU.add))
                spread.done(dve, step.pair(), back=2)
                yield then(dve.tensor_copy(pair_row[:, buf, :], r_row[:, :]), PLACED)
            def weigh_pairs(step):
                if step.offset % 2 == 0:
                    return
                steps[0] = PLACED
                then = counter(step.pair())
                exped.done(dve, step.pair())
                yield then(dve.tensor_reduce(r_sum, te(r_exp), AX.X, ALU.add))
                buf = step.pair().buf
                pair_weight = pair_val[:, :, :, :].bitcast(F32)[:, buf, :, :]
                yield then(dve.reciprocal(r_rank, r_sum))
                dve.tensor_scalar(pair_weight[:, 0:BT, 1], r_rank, 1.0 / SCALE, None, ALU.mult)
                yield then(dve.scalar_tensor_tensor(out=pair_weight[:, BT:2 * BT, 1], in0=r_exp2, scalar=1.0 / SCALE,
                                              in1=r_rank, op0=ALU.mult, op1=ALU.mult))
                flat = tokens[:, :, :, :].rearrange("p k w s -> p (k w s)")
                yield then(dve.tensor_scalar(flat, flat, float(GROUP), None, ALU.add))
                yield then(dve.tensor_copy(pair_val[:, buf, :, 0], flat), ROUTED)

            track = {statistics: "N", reciprocal_root: "N", low: "R", recur: "R", add_x: "R", prepare: "R",
                     centre: "T", pick: "T", place_pairs: "T", weigh_pairs: "T"}
            run_steps(dve, GROUPS, [(0, statistics), (0, reciprocal_root), (2, low), (6, add_x), (1, prepare),
                                    (3, recur), (4, centre), (4, pick), (5, place_pairs), (5, weigh_pairs)],
                      unroll=4, emit_step=take_turns)

            run_steps(dve, E, [(0, w2_low)])

            planned = [0]

            def plan(instruction):
                planned[0] += 1
                instruction.then_inc(s_plan, 1)
                dve.wait_ge(s_plan, planned[0])

            plan(dve.tensor_tensor(r_cnt, next_row[0:1, :], list_start[0:1, :], ALU.subtract))
            plan(dve.tensor_scalar(r_int, r_cnt, float(TILE - 1), None, ALU.add))
            plan(dve.tensor_scalar(r_int2, r_int, TILE.bit_length() - 1, None, ALU.logical_shift_right))
            plan(dve.tensor_copy(r_tiles, r_int2))
            plan(dve.tensor_tensor_scan(r_end, one_row[:, :], r_tiles, 0.0, ALU.mult, ALU.add))
            ends = r_end[0:1, 0:E - 1].unsqueeze(1).to_broadcast([1, N_TILES, E - 1])
            plan(dve.tensor_tensor(r_cmp[:, :, :], tile_no[0:1, :].unsqueeze(2).to_broadcast([1, N_TILES, E - 1]), ends,
                                   ALU.is_ge))
            plan(dve.tensor_reduce(r_te[:, :], r_cmp[:, :, :], AX.X, ALU.add))
            plan(dve.tensor_tensor(r_cmp[:, :, :], r_cmp[:, :, :], ends, ALU.mult))
            plan(dve.tensor_reduce(r_first[:, :], r_cmp[:, :, :], AX.X, ALU.max))
            plan(dve.tensor_scalar(expert_off[:, :], r_te[:, :], float(WCHUNK), None, ALU.mult))
            plan(dve.tensor_tensor(r_first[:, :], tile_no[:, :], r_first[:, :], ALU.subtract))
            plan(dve.tensor_scalar(r_off[:, :], r_te[:, :], float(TOKENS), None, ALU.mult))
            plan(dve.scalar_tensor_tensor(out=tile_row[:, :], in0=r_first[:, :], scalar=float(TILE), in1=r_off[:, :],
                                          op0=ALU.mult, op1=ALU.add))
            assert planned[0] == PLANNED

            def g_move(step):
                g_turned.done(dve, step)
                hidden.done(dve, step, back=2)
                for h in range(2):
                    dve.tensor_copy(tT[step.buf][:, h, :, :].rearrange("p k t -> p (k t)"),
                                    bank16(6 + step.buf)[:, h * KC * TILE:(h + 1) * KC * TILE])\
                       .then_inc(g_moved.sem, 1)

            def h_split(step):
                for q in range(2):
                    gelued.done(dve, step, q + 1)
                    if q == 0:
                        y_made.done(dve, step, back=2)
                    high_part = h16[step.buf][:, 0, 2 * q:2 * q + 2, :].rearrange("p f t -> p (f t)")
                    low_part = h16[step.buf][:, 1, 2 * q:2 * q + 2, :].rearrange("p f t -> p (f t)")
                    dve.tensor_scalar(high_part, h32[step.buf][q], X_SCALE, None, ALU.mult).then_inc(hhi.sem, 1)
                    hhi.done(dve, step, q + 1)
                    dve.scalar_tensor_tensor(out=low_part, in0=h32[step.buf][q], scalar=X_SCALE, in1=high_part,
                                             op0=ALU.mult, op1=ALU.subtract).then_inc(hlo.sem, 1)

            run_steps(dve, N_TILES, [(0, g_move), (1, h_split)])


def kernel(**inputs):
    import numpy as np
    import concourse.bacc as bacc
    from concourse.bass_utils import run_bass_kernel_spmd

    def arr(name):
        return np.asarray(inputs[name])

    w1 = arr("L0_ffn_w1").reshape(E, F, KC, P).transpose(3, 0, 2, 1).reshape(P, E, KC * F)
    w2 = arr("L0_ffn_w2").reshape(E, D, FC, P).transpose(3, 0, 2, 1).reshape(P, E, FC * D)
    laid_out = {
        "x": arr("L0_attn_x"), "wa": arr("L0_attn_Wa"), "wb": arr("L0_attn_Wb"), "wc": arr("L0_attn_Wc"),
        "wd": arr("L0_attn_Wd"), "wy": arr("L0_attn_Wy"),
        "cols": np.stack([arr("L0_attn_ba"), arr("L0_attn_bb"), arr("L0_attn_bc")], axis=1),
        "rows": np.stack([arr("L0_attn_by"), arr("L0_attn_bd")]),
        "gate": arr("L0_ffn_gate_w").reshape(E, KC, P).transpose(2, 1, 0),
        "gamma_beta": np.stack([arr("L0_ffn_ln_gamma"), arr("L0_ffn_ln_beta")]).reshape(2, KC, P).transpose(2, 0, 1),
        "experts": np.concatenate([w1, w2], axis=1),
    }
    nc = bacc.Bacc("TRN2", target_bir_lowering=False, num_devices=1)
    arrays, args = {}, []
    for name, a in laid_out.items():
        a = np.ascontiguousarray(a)
        arrays[f"in_{name}"] = a
        args.append(nc.dram_tensor(f"in_{name}", a.shape, mybir.dt.from_np(a.dtype), kind="ExternalInput").ap())
    args.append(nc.dram_tensor("out_0", (BATCH, SEQ, D), F32, kind="ExternalOutput").ap())
    build(nc, *args)
    return run_bass_kernel_spmd(nc, [arrays], core_ids=[0]).results[0]["out_0"]
```

```python
from contextlib import ExitStack
from functools import partial
from itertools import chain, cycle

import concourse.bass as bass
from concourse import mybir

F32 = mybir.dt.float32
F16 = mybir.dt.float16
I32 = mybir.dt.int32
ALU = mybir.AluOpType
ACT = mybir.ActivationFunctionType
AX = mybir.AxisListType

P = 128
BATCH, SEQ, D = 4, 2048, 256
TOKENS = BATCH * SEQ
N = 64
E, F, TOP = 8, 512, 2
KC = D // P
FC = F // P
GROUP = 512
SUB = GROUP // P
GROUPS = TOKENS // GROUP
PAIRS_OF_GROUPS = GROUPS // 2
SEQ_GROUPS = SEQ // GROUP
BATCHES = PAIRS_OF_GROUPS
BT = 2 * SUB
TT = TOKENS // P
PAIRS = TOP * BT
TILE = 256
TSUB = TILE // P
N_TILES = (TOP * TOKENS + E * (TILE - 1)) // TILE
LIST_ROWS = (E - 1) * TOKENS + N_TILES * TILE
FILL = LIST_ROWS // P
FIRST_TILES = 6
NO_TOKEN = 1 << 20
EPS = 1e-5
NEWTON = 17
MAGIC = 0x5F3759DF
X_SCALE, W_SCALE = 8.0, 64.0
SCALE = X_SCALE * W_SCALE
WCHUNK = 2 * KC * F
GATE_SPLIT, ALL_SPLIT, BIASED, PLANNED = 2, 17, 17, 13
LOGITS, CENTRED, SECOND, CHOSEN, COUNTS_READ, PLACED, ROUTED = 1, 4, 9, 14, 16, 25, 29
LOW_ROW = 32
PARTS = ((0, 0), (0, 1), (1, 0))

END = object()


class Step:

    def __init__(self, turn, offset, unroll=2):
        self.turn, self.offset, self.unroll = turn, offset, unroll
        self.i = turn * unroll + offset
        self.buf = offset % 2
        self.half = turn * (unroll // 2) + offset // 2

    def pair(self):
        return Step(self.turn, self.offset // 2, self.unroll // 2)

    def plus(self, n):
        return Step(self.turn, self.offset + n, self.unroll)


def only(parity, emit):
    def chosen(step):
        if step.offset % 2 == parity:
            emit(step)
    return chosen


def run_steps(eng, count, stages, unroll=2, peel=0, emit_step=None):
    last_lag = max(lag for lag, _ in stages)
    head = -(-max(last_lag, peel) // unroll) * unroll
    turns = (count - head) // unroll

    def one_step(work):
        if emit_step is not None:
            emit_step(work)
        else:
            for emit, step in work:
                emit(step)

    def straight(g):
        one_step([(emit, Step(0, g - lag, unroll)) for lag, emit in stages if 0 <= g - lag < count])

    for g in range(head):
        straight(g)
    with eng.Fori(0, turns) as turn:
        for place in range(unroll):
            one_step([(emit, Step(turn, head + place - lag, unroll)) for lag, emit in stages])
    for g in range(head + turns * unroll, count + last_lag):
        straight(g)


def park(eng, mark):
    eng.sem_inc(mark, 1)


class Signal:

    def __init__(self, sem, per=1, depth=2):
        self.sem, self.per, self.depth = sem, per, depth

    def give_credit(self, eng):
        if self.depth:
            eng.sem_inc(self.sem, self.per * self.depth)

    def done(self, eng, step, k=None, back=0):
        assert back <= self.depth
        eng.wait_ge(self.sem, (step.i + (self.depth - back)) * self.per + (self.per if k is None else k))

    def all(self, eng, count):
        eng.wait_ge(self.sem, (count + self.depth) * self.per)


class DmaSignal:

    def __init__(self, sems, per=1, credit=True):
        self.sems, self.per, self.credit = sems, 16 * per, int(credit)

    def give_credit(self, eng):
        if self.credit:
            for sem in self.sems:
                eng.sem_inc(sem, self.per)

    def inc(self, dma, step):
        dma.then_inc(self.sems[step.buf], 16)

    def done(self, eng, step):
        turns = step.half + 1 + self.credit
        if not isinstance(turns, int) or turns > 0:
            eng.wait_ge(self.sems[step.buf], turns * self.per)

    def free(self, eng, step):
        turns = step.half + self.credit
        if not isinstance(turns, int) or turns > 0:
            eng.wait_ge(self.sems[step.buf], turns * self.per)

    def all(self, eng, count):
        for buf, sem in enumerate(self.sems):
            eng.wait_ge(sem, ((count + 1 - buf) // 2 + self.credit) * self.per)


def build(nc, x, wa, wb, wc, wd, wy, cols, rows, gate, gamma_beta, experts, out):
    x_tok = x.rearrange("(w b) (c p) d -> p w (b c) d", w=2, p=P)
    out_tok = out.rearrange("(w b) (c p) d -> p w (b c) d", w=2, p=P)
    out_rows = out.rearrange("b t d -> (b t) d")
    xn_dram = nc.dram_tensor("xn_rows", [TOKENS, 2 * D], F16, kind="Internal").ap()
    list_dram = nc.dram_tensor("expert_lists", [LIST_ROWS, 2], I32, kind="Internal").ap()
    xn_tok = xn_dram.rearrange("(w c p) d -> p w c d", w=2, p=P)

    with ExitStack() as ctx:
        def sb(name, shape, dt):
            return ctx.enter_context(nc.sbuf_tensor(name, shape, dt))

        def sem(name):
            return ctx.enter_context(nc.semaphore(name))

        def signal(name, per=1, depth=2):
            return Signal(sem(name), per, depth)

        def dma_signal(name, per=1, credit=True):
            return DmaSignal([sem(f"{name}_{b}") for b in range(2)], per, credit)

        w16 = sb("w16", [P, 2 * E, WCHUNK], F16)
        w16_flat = w16[:, :, :].rearrange("p e w -> p (e w)")
        ident = sb("ident", [P, P], F16)
        before = sb("before", [P, P], F16)
        ones16 = sb("ones16", [P, P], F16)
        keep = sb("keep", [P, E, BT], F32)
        rank = sb("rank", [P, E], F32)
        list_start = sb("list_start", [P, E], F32)
        one_row = sb("one_row", [1, E], F32)
        tile_no = sb("tile_no", [1, N_TILES], F32)
        fill = sb("fill", [P, FILL, 2], I32)
        abc32 = sb("abc32", [P, KC, 3, N], F32)
        abc16 = sb("abc16", [P, 2, KC, 2, 3 * N], F16)
        wd32 = sb("wd32", [P, KC, D], F32)
        wd16 = sb("wd16", [P, 2, KC, D], F16)
        wy32 = sb("wy32", [2 * N, D], F32)
        wy16 = sb("wy16", [2 * N, 2, 2, D], F16)
        by_row, bd_row, bias_row = (sb(n, [LOW_ROW + 1, D], F32) for n in ("by_row", "bd_row", "bias_row"))
        bias_high = sb("bias_high", [LOW_ROW + 1, D], F16)
        bias16 = sb("bias16", [LOW_ROW + 1, D], F16)
        eights = sb("eights", [LOW_ROW + 1, P], F16)
        gate32 = sb("gate32", [P, KC, E], F32)
        gated = sb("gated", [P, KC, E], F32)
        gate16 = sb("gate16", [P, 2, KC, E], F16)
        gb = sb("gb", [P, 2, KC], F32)
        beta_b = sb("beta_b", [P, KC, P], F32)
        bias8 = sb("bias8", [P, E], F32)
        col = sb("col", [2 * N, 3], F32)
        ba_half, bb_s, half, minus_one = (sb(n, [2 * N, 1], F32) for n in ("ba_half", "bb_s", "half", "minus_one"))
        carry = sb("carry", [2 * N, PAIRS_OF_GROUPS], F32)
        xin = sb("xin", [P, 2, 2 * SUB, D], F32)
        x_res = sb("x_res", [P, 2, SUB, D], F32)
        x8 = sb("x8", [P, 2, SUB, D], F32)
        out_sb = sb("out_sb", [P, 2, SUB, D], F32)
        xn16 = sb("xn16", [P, 2, SUB, 2, D], F16)
        xT = sb("xT", [P, 4, 2, KC, GROUP], F16)
        w_stage = sb("w_stage", [P, 2, WCHUNK // 2], F32)
        w_scale, zero = sb("w_scale", [P, 1], F32), sb("zero", [P, 1], F32)
        bn = sb("bn", [P, 2 * SUB, 6], F32)
        mv = sb("mv", [P, 2 * SUB, 2], F32)
        ve, nh, nq, ny, nz = (sb(n, [P, 2, 2 * SUB], F32) for n in ("ve", "nh", "nq", "ny", "nz"))
        root = sb("root", [P, 2 * SUB], F32)
        router_norm = sb("router_norm", [P, TT], F32)
        rs8 = sb("rs8", [P, 2, 2 * SUB], F32)
        nmr8 = sb("nmr8", [P, 2, 2 * SUB], F32)
        tanh_a = sb("tanh_a", [2 * N, GROUP], F32)
        a_sb = sb("a_sb", [2 * N, 2, GROUP], F32)
        m_sb = sb("m_sb", [2 * N, 2, GROUP], F32)
        b_sb = sb("b_sb", [2 * N, 2, GROUP], F32)
        c_sb = sb("c_sb", [2 * N, 2, GROUP], F32)
        u_sb = sb("u_sb", [2 * N, GROUP], F32)
        initial = sb("initial", [2 * N, 1], F32)
        state = sb("state", [2 * N, 2, GROUP], F32)
        cs8 = sb("cs8", [2 * N, GROUP], F32)
        cs16 = sb("cs16", [2 * N, 2, 2, GROUP], F16)
        (r_logit, r_exp, r_one1, r_one2, r_rest, r_tmp, r_tot, r_run, r_slot) = (
            sb(n, [P, BT * E], F32)[:, :] for n in ("r_logit", "r_exp", "r_one1", "r_one2", "r_rest", "r_tmp",
                                                     "r_tot", "r_run", "r_slot"))
        chosen16 = sb("chosen16", [P, BT * E], F16)
        r_max1, r_max2, r_exp2, r_rank, r_sum = (
            sb(n, [P, BT], F32)[:, :] for n in ("r_max1", "r_max2", "r_exp2", "r_rank", "r_sum"))
        next_row = sb("next_row", [P, E], F32)
        pair_val = sb("pair_val", [P, 2, PAIRS, 2], I32)
        r_row = sb("r_row", [P, PAIRS], F32)
        pair_row = sb("pair_row", [P, 2, PAIRS], I32)
        r_int, r_int2 = (sb(n, [1, E], I32)[:, :] for n in ("r_int", "r_int2"))
        r_cnt, r_tiles, r_end = (sb(n, [1, E], F32)[:, :] for n in ("r_cnt", "r_tiles", "r_end"))
        r_cmp = sb("r_cmp", [1, N_TILES, E - 1], F32)
        r_te, r_first, r_off = (sb(n, [1, N_TILES], F32) for n in ("r_te", "r_first", "r_off"))
        expert_off = sb("expert_off", [1, N_TILES], I32)
        tile_row = sb("tile_row", [1, N_TILES], I32)
        table = sb("table", [P, N_TILES * TSUB, 2], I32)
        gidx = sb("gidx", [P, 2, TSUB], I32)
        sidx = sb("sidx", [P, TSUB], I32)
        xg = [[sb(f"xg{b}{s}", [P, 2 * D], F16)[:, :] for s in range(TSUB)] for b in range(2)]
        xT_flat = xT[:, :, :, :, :].rearrange("p b h k t -> p (b h k t)")
        xin_flat = xin[:, :, :, :].rearrange("p b s d -> p (b s d)")
        split_size, h32_size, tT_size, ys_size = 2 * FC * TILE, 4 * TILE, 2 * KC * TILE // 2, TSUB * D
        h16 = [xT_flat[:, b * split_size:(b + 1) * split_size].rearrange("p (h f t) -> p h f t", h=2, f=FC)
               for b in range(2)]
        h32 = [[xT_flat[:, 2 * split_size + (2 * b + q) * h32_size:2 * split_size + (2 * b + q + 1) * h32_size]
                .bitcast(F32) for q in range(2)] for b in range(2)]
        tT = [xin_flat[:, b * tT_size:(b + 1) * tT_size].bitcast(F16).rearrange("p (h k t) -> p h k t", h=2, k=KC)
              for b in range(2)]
        ys = [xin_flat[:, 2 * tT_size + b * ys_size:2 * tT_size + (b + 1) * ys_size]
              .rearrange("p (s d) -> p s d", s=TSUB) for b in range(2)]

        ps = ctx.enter_context(nc.psum_tensor("ps", [P, 8, 512], F32))
        B_TURN, B_AB, B_C, B_ROUTE, B_SUM = 0, 2, 4, 5, 6
        SCORE_COL, COUNT_COL = 0, BT * E

        def bank(b):
            return ps[:, b, :]

        def bank16(b):
            return ps[:, b, :].bitcast(F16)

        s_ident, s_const, s_small, s_betab, s_fill, s_filled, s_prep = (sem(n) for n in (
            "s_ident", "s_const", "s_small", "s_betab", "s_fill", "s_filled", "s_prep"))
        s_bias8 = sem("s_bias8")
        s_ld = [sem(f"s_ld{j}") for j in range(14)]
        x_in, x_again = dma_signal("x_in", 2), dma_signal("x_again")
        stats, newton = signal("stats", 2, 0), signal("newton", NEWTON, 0)
        x8_made, hi_made = signal("x8_made", depth=3), signal("hi_made")
        lo_made = signal("lo_made")
        stored = dma_signal("stored")
        turned = signal("turned", 2)
        moved = signal("moved", 2)
        scored = signal("scored")
        projected = signal("projected", 2)
        gates = signal("gates", 7)
        u_made, init_made, s_made, cs_made, cshi, cslo = (
            signal(n) for n in ("u_made", "init_made", "s_made", "cs_made", "cshi", "cslo"))
        summed = signal("summed", 2, 4)
        added = signal("added", 2)
        out_put = dma_signal("out_put")
        w1_in = dma_signal("w1_in", credit=False)
        w1_scaled, w1_hi, w1_lo = signal("w1_scaled"), signal("w1_hi"), signal("w1_lo")
        w2_in = dma_signal("w_in")
        w2_hi, w2_lo = signal("w2_hi"), signal("w2_lo")
        route = signal("route", ROUTED, 0)
        exped = signal("exped", 2, 0)
        counted = signal("counted", 1, 0)
        s_scatter = [sem(f"s_scatter_{b}") for b in range(2)]
        spread = signal("spread", 1, 2)
        s_plan = sem("s_plan")
        fetched = dma_signal("fetched")
        gi_made = signal("gi_made")
        gathered = dma_signal("gathered", TSUB, credit=False)
        g_turned, g_moved = signal("g_turned"), signal("g_moved", 2)
        hidden = signal("hidden", 2)
        gelued = signal("gelued", 2)
        hhi, hlo = signal("hhi", 2), signal("hlo", 2)
        y_made, y_out = signal("y_made"), signal("y_out")
        si_made = signal("si_made")
        put_back = dma_signal("put_back", TSUB, credit=False)
        s_mark = sem("s_mark")
        s_clear = sem("s_clear")
        every = [fetched, x_in, x_again, x8_made, hi_made, lo_made, stored, turned, moved, scored, projected, gates,
                 u_made, init_made, s_made, cs_made, cshi, cslo, summed, added, out_put, w1_scaled, w1_hi, w1_lo,
                 w2_in, w2_hi, w2_lo, spread, gi_made,
                 g_turned, g_moved, hidden, gelued, hhi, hlo, y_made, y_out, si_made]

        block = ctx.enter_context(nc.Block())

        @block.sync
        def _(sp):
            def half_rows(tok, step):
                return tok[:, step.buf, bass.ds(step.half * SUB, SUB), :]

            def load_x(step):
                if step.offset % 2 == 0:
                    x8_made.done(sp, step, back=3)
                    park(sp, s_mark)
                    for w in range(2):
                        x_in.inc(sp.dma_start(xin[:, step.pair().buf, w * SUB:(w + 1) * SUB, :],
                                              half_rows(x_tok, step.plus(w))), step.pair())

            def load_w2(step):
                w1_lo.all(sp, E)
                w2_lo.done(sp, step, back=2)
                park(sp, s_mark)
                w2_in.inc(sp.dma_start(w_stage[:, step.buf:step.buf + 1, :], experts[:, bass.ds(step.i + E, 1), :]),
                          step)

            def load_first_w2(step):
                if isinstance(step.i, int) and step.i >= GROUPS - 2:
                    load_w2(Step(0, step.i - (GROUPS - 2)))

            def store_xn(step):
                lo_made.done(sp, step)
                park(sp, s_mark)
                stored.inc(sp.dma_start(half_rows(xn_tok, step),
                                        xn16[:, step.buf, :, :, :].rearrange("p s h d -> p s (h d)")), step)

            def load_x_again(step):
                added.done(sp, step, back=2)
                park(sp, s_mark)
                x_again.inc(sp.dma_start(x_res[:, step.buf, :, :], half_rows(x_tok, step)), step)

            def store_out(step):
                added.done(sp, step)
                park(sp, s_mark)
                out_put.inc(sp.dma_start(half_rows(out_tok, step), out_sb[:, step.buf, :, :]), step)

            x8_made.give_credit(sp)
            x_in.give_credit(sp)
            load_x(Step(0, 0, 4))
            for s in every:
                if s is not x8_made and s is not x_in:
                    s.give_credit(sp)
            sp.dma_start(gate32[:, :, :], gate).then_inc(s_ld[0], 16)
            sp.dma_start(gb[:, :, :], gamma_beta).then_inc(s_ld[1], 16)
            for w, source in enumerate((wa, wb, wc)):
                sp.dma_start(abc32[:, :, w, :], source.rearrange("(k p) n -> p k n", p=P)).then_inc(s_ld[2 + w], 16)
            sp.wait_ge(s_fill, 2)
            sp.dma_start(list_dram.rearrange("(p c) v -> p c v", p=P), fill[:, :, :]).then_inc(s_filled, 16)

            def load_x_once(step):
                if step.offset > 0 or not isinstance(step.i, int):
                    load_x(step)

            run_steps(sp, GROUPS, [(0, load_x_once), (3, store_xn), (7, store_out), (5, load_x_again),
                                   (5, load_first_w2)], unroll=4)
            run_steps(sp, E - 2, [(0, lambda step: load_w2(step.plus(2)))])

            sp.wait_ge(s_plan, PLANNED)
            spread.all(sp, BATCHES)

            def fetch(step):
                fetched.free(sp, step)
                row = sp.value_load(tile_row[0:1, bass.ds(step.i, 1)], min_val=0, max_val=LIST_ROWS - TILE)
                fetched.inc(sp.dma_start(table[:, bass.ds(step.i * TSUB, TSUB), :],
                                         list_dram[bass.ds(row, TILE), :].rearrange("(p s) v -> p s v", s=TSUB)), step)

            run_steps(sp, N_TILES, [(0, fetch)])
            out_put.all(sp, GROUPS)
            put_back.all(sp, N_TILES)

        @block.gpsimd
        def _(pool):
            pool.memset(ident[:, :], 0.0).then_inc(s_ident, 1)
            pool.memset(ones16[:, :], 1.0).then_inc(s_ident, 1)
            pool.wait_ge(s_ident, 2)
            pool.affine_select(out=ident[:, :], in_=ident[:, :], compare_op=ALU.not_equal, fill=1.0, base=0,
                               pattern=[[-1, P]], channel_multiplier=1).then_inc(s_ident, 1)
            pool.affine_select(out=before[:, :], in_=ones16[:, :], compare_op=ALU.is_gt, fill=0.0, base=0,
                               pattern=[[1, P]], channel_multiplier=-1).then_inc(s_const, 1)
            pool.memset(keep[:, :, :], 1.0).then_inc(s_const, 1)
            pool.iota(rank[:, :], [[-1, E]], base=E, channel_multiplier=0,
                      allow_small_or_imprecise_dtypes=True).then_inc(s_const, 1)
            pool.iota(tile_no[0:1, :], [[1, N_TILES]], base=0, channel_multiplier=0,
                      allow_small_or_imprecise_dtypes=True).then_inc(s_const, 1)
            for buf in range(2):
                for k in range(TOP):
                    for w in range(2):
                        c = k * BT + w * SUB
                        pool.iota(pair_val[:, buf, c:c + SUB, 0], [[P, SUB]], channel_multiplier=1,
                                  base=w * (TOKENS // 2) + (buf - 2) * GROUP).then_inc(s_const, 1)
            pool.iota(list_start[:, :], [[TOKENS, E]], base=0, channel_multiplier=0,
                      allow_small_or_imprecise_dtypes=True).then_inc(s_const, 1)
            pool.iota(next_row[:, :], [[TOKENS, E]], base=0, channel_multiplier=0,
                      allow_small_or_imprecise_dtypes=True).then_inc(s_const, 1)
            pool.memset(w_scale[:, :], W_SCALE).then_inc(s_const, 1)
            pool.memset(zero[:, :], 0.0).then_inc(s_const, 1)
            pool.memset(fill[:, :, :], 0).then_inc(s_fill, 1)
            pool.wait_ge(s_const, 16)
            pool.wait_ge(s_fill, 1)
            pool.memset(keep[:, :, 0:1], 0.0).then_inc(s_const, 1)
            pool.memset(fill[:, :, 0], NO_TOKEN).then_inc(s_fill, 1)
            pool.wait_ge(s_fill, 2)
            for b in range(2):
                for s in range(TSUB):
                    pool.memset(xg[b][s], 0.0).then_inc(s_clear, 1)
            pool.wait_ge(s_clear, 2 * TSUB)

            def everywhere(column):
                return column[:, :].unsqueeze(2).to_broadcast([P, 1, WCHUNK // 2])

            def load_w1(step):
                w1_lo.done(pool, step, back=2)
                park(pool, s_mark)
                w1_in.inc(pool.dma_start(w_stage[:, step.buf, :], experts[:, bass.ds(step.i, 1), :]), step)

            def split_w1(step):
                scaled = w_stage[:, step.buf:step.buf + 1, :]
                high_part = w16[:, bass.ds(step.i, 1), 0:WCHUNK // 2]
                w1_in.done(pool, step)
                park(pool, s_mark)
                pool.tensor_tensor(scaled, scaled, everywhere(w_scale), ALU.mult).then_inc(w1_scaled.sem, 1)
                w1_scaled.done(pool, step)
                park(pool, s_mark)
                pool.tensor_tensor(high_part, scaled, everywhere(zero), ALU.add).then_inc(w1_hi.sem, 1)
                w1_hi.done(pool, step)
                park(pool, s_mark)
                pool.tensor_tensor(w16[:, bass.ds(step.i, 1), WCHUNK // 2:WCHUNK], scaled, high_part, ALU.subtract)\
                    .then_inc(w1_lo.sem, 1)

            run_steps(pool, E, [(0, load_w1), (1, split_w1)])
            w1_lo.all(pool, E)

            pool.wait_ge(s_filled, 16)
            def scatter(batch):
                route.done(pool, batch)
                park(pool, s_mark)
                for j in range(PAIRS):
                    pool.indirect_dma_start(list_dram[:, :],
                                            bass.IndirectOffsetOnAxis(ap=pair_row[:, batch.buf, j:j + 1], axis=0),
                                            pair_val[:, batch.buf, j, :], None).then_inc(s_scatter[batch.buf], 16)

            def scattered(batch):
                pool.wait_ge(s_scatter[batch.buf], (batch.half + 1) * (16 * PAIRS))
                pool.sem_inc(spread.sem, 1)

            run_steps(pool, BATCHES, [(0, scatter), (1, scattered)])

            stored.all(pool, GROUPS)

            def gather(step):
                gathered.free(pool, step)
                fetched.done(pool, step)
                park(pool, s_mark)
                pool.tensor_copy(gidx[:, step.buf, :], table[:, bass.ds(step.i * TSUB, TSUB), 0]).then_inc(gi_made.sem, 1)
                g_turned.done(pool, step, back=2)
                gi_made.done(pool, step)
                park(pool, s_mark)
                for s in range(TSUB):
                    gathered.inc(pool.indirect_dma_start(
                        xg[step.buf][s], None, xn_dram[:, :],
                        bass.IndirectOffsetOnAxis(ap=gidx[:, step.buf, s:s + 1], axis=0),
                        bounds_check=TOKENS - 1, oob_is_err=False), step)

            def add_back(step):
                if step.offset > 0:
                    put_back.done(pool, step.plus(-1))
                else:
                    out_put.all(pool, GROUPS)
                park(pool, s_mark)
                pool.tensor_copy(sidx[:, :], table[:, bass.ds(step.i * TSUB, TSUB), 0]).then_inc(si_made.sem, 1)
                y_out.done(pool, step)
                si_made.done(pool, step)
                park(pool, s_mark)
                for s in range(TSUB):
                    put_back.inc(pool.indirect_dma_start(
                        out_rows, bass.IndirectOffsetOnAxis(ap=sidx[:, s:s + 1], axis=0),
                        ys[step.buf][:, s, :], None, bounds_check=TOKENS - 1, oob_is_err=False,
                        compute_op=ALU.add), step)

            run_steps(pool, N_TILES, [(0, gather), (4, add_back)], peel=FIRST_TILES)

        @block.tensor
        def _(pe):
            pe.wait_ge(s_ident, 3)

            def transposes(step):
                lo_made.done(pe, step)
                for h in range(2):
                    moved.done(pe, step, h + 1, back=1)
                    dst = bank16(B_TURN + h).rearrange("p (k t) -> p k t", k=KC)
                    for k in range(KC):
                        for s in range(SUB):
                            t = pe.transpose(dst[:, k, s * P:(s + 1) * P], xn16[:, step.buf, s, h, k * P:(k + 1) * P],
                                             ident[:, :])
                    t.then_inc(turned.sem, 1)

            def scores(step):
                if step.offset > 1 or not isinstance(step.i, int):
                    route.done(pe, step.pair().plus(-1), COUNTS_READ if step.offset % 2 else LOGITS)
                elif step.offset == 0:
                    pe.wait_ge(s_small, GATE_SPLIT)
                    pe.wait_ge(s_prep, BIASED)
                col0 = SCORE_COL + step.buf * (SUB * E)
                for s in range(SUB):
                    n = 0
                    for k in range(KC):
                        for a, b in PARTS:
                            m = pe.matmul(bank(B_ROUTE)[:, col0 + s * E:col0 + (s + 1) * E],
                                          xT[:, step.offset % 4, a, k, s * P:(s + 1) * P], gate16[:, b, k, :],
                                          start=(n == 0), stop=(n == 2 * KC + 1))
                            n += 1
                m.then_inc(scored.sem, 1)

            def project(step):
                moved.done(pe, step)
                if step.offset == 0 and isinstance(step.i, int):
                    pe.wait_ge(s_small, ALL_SPLIT)
                w = step.buf
                gates.done(pe, step.pair(), w + 5, back=1)
                for j, cols16 in enumerate((w * N, (1 - w) * N)):
                    if j == 1 and w == 0:
                        gates.done(pe, step.pair(), back=1)
                    n = 0
                    for k in range(KC):
                        for a, b in PARTS:
                            m = pe.matmul(bank((B_AB + w, B_C)[j]), abc16[:, b, k, j, cols16:cols16 + 2 * N],
                                          xT[:, step.offset % 4, a, k, :], start=(n == 0 and (j, w) != (1, 1)),
                                          stop=(n == 2 * KC + 1 and (j, w) != (1, 0)))
                            n += 1
                    m.then_inc(projected.sem, 1)

            def sums(step):
                def from_x(s):
                    n = 0
                    for k in range(KC):
                        for a, b in PARTS:
                            pe.matmul(dst[s], xT[:, step.offset % 4, a, k, s * P:(s + 1) * P], wd16[:, b, k, :],
                                      start=(n == 0), stop=False)
                            n += 1
                    pe.matmul(dst[s], eights[:, :], bias16[:, :], start=False, stop=False)

                def from_state(s):
                    for n, (a, b) in enumerate(PARTS):
                        m = pe.matmul(dst[s], cs16[:, step.pair().buf, a, s * P:(s + 1) * P], wy16[:, step.buf, b, :],
                                      start=False, stop=(n == 2))
                    return m

                dst = [bank(B_SUM + s // 2)[:, (s % 2) * D:(s % 2 + 1) * D] for s in range(SUB)]
                for j in range(2):
                    added.done(pe, step, j + 1, back=1)
                    from_x(2 * j)
                cslo.done(pe, step.pair())
                for j in range(2):
                    from_state(2 * j)
                    from_x(2 * j + 1)
                    from_state(2 * j + 1).then_inc(summed.sem, 1)

            def counts(step):
                if step.offset % 2:
                    route.done(pe, step.pair(), CHOSEN)
                    for j, matrix in enumerate((before, ones16)):
                        col0 = COUNT_COL + j * BT * E
                        m = pe.matmul(bank(B_ROUTE)[:, col0:col0 + BT * E], matrix[:, :], chosen16[:, :], start=True,
                                      stop=True)
                    m.then_inc(counted.sem, 1)

            pe.wait_ge(s_betab, 1)
            for k in range(KC):
                m = pe.matmul(bank(B_ROUTE)[:, 0:E], beta_b[:, k, :], gate32[:, k, :], start=(k == 0), stop=(k == KC - 1))
            m.then_inc(s_bias8, 1)
            pe.wait_ge(s_const, 17)
            run_steps(pe, GROUPS, [(5, counts), (3, only(1, project)), (2, transposes), (3, only(0, project)),
                                   (3, scores), (5, sums)], unroll=4)

            added.all(pe, GROUPS)
            w1_lo.all(pe, E)
            w2_lo.all(pe, E)
            pe.wait_ge(s_plan, PLANNED)

            def g_transposes(step):
                gathered.done(pe, step)
                g_moved.done(pe, step, back=2)
                dst = bank16(6 + step.buf).rearrange("p (h k t) -> p h k t", h=2, k=KC)
                for s in range(TSUB):
                    for h in range(2):
                        for k in range(KC):
                            t = pe.transpose(dst[:, h, k, s * P:(s + 1) * P],
                                             xg[step.buf][s][:, h * D + k * P:h * D + (k + 1) * P], ident[:, :])
                t.then_inc(g_turned.sem, 1)

            def up(step):
                off = pe.value_load(expert_off[0:1, bass.ds(step.i, 1)], min_val=0, max_val=(E - 1) * WCHUNK)
                g_moved.done(pe, step)
                for q in range(2):
                    gelued.done(pe, step, q + 1, back=2)
                    park(pe, s_mark)
                    for f in (2 * q, 2 * q + 1):
                        dst = bank(2 * step.buf + q)[:, (f % 2) * TILE:(f % 2 + 1) * TILE]
                        n = 0
                        for k in range(KC):
                            for a, b in PARTS:
                                m = pe.matmul(dst, w16_flat[:, bass.ds(off + ((b * KC + k) * F + f * P), P)],
                                              tT[step.buf][:, a, k, :], start=(n == 0), stop=(n == 2 * KC + 1))
                                n += 1
                    m.then_inc(hidden.sem, 1)

            def down(step):
                off = pe.value_load(expert_off[0:1, bass.ds(step.i, 1)], min_val=0, max_val=(E - 1) * WCHUNK)
                hlo.done(pe, step)
                y_out.done(pe, step, back=2)
                park(pe, s_mark)
                for s in range(TSUB):
                    n = 0
                    for f in range(FC):
                        for b, a in PARTS:
                            m = pe.matmul(bank(4 + step.buf)[:, s * D:(s + 1) * D],
                                          h16[step.buf][:, a, f, s * P:(s + 1) * P],
                                          w16_flat[:, bass.ds(off + (E * WCHUNK + (b * FC + f) * D), D)],
                                          start=(n == 0), stop=(n == 3 * FC - 1))
                            n += 1
                m.then_inc(y_made.sem, 1)

            run_steps(pe, N_TILES, [(0, g_transposes), (1, up), (2, down)])

        @block.scalar
        def _(act):
            act.dma_start(wd32[:, :, :], wd.rearrange("(k p) n -> p k n", p=P)).then_inc(s_ld[5], 16)
            for w in range(2):
                act.dma_start(wy32[w * N:(w + 1) * N, :], wy).then_inc(s_ld[6 + w], 16)
                act.dma_start(col[w * N:(w + 1) * N, :], cols).then_inc(s_ld[8 + w], 16)
            for j, row in enumerate((0, LOW_ROW)):
                act.dma_start(by_row[row:row + 1, :], rows[0:1, :]).then_inc(s_ld[10 + j], 16)
                act.dma_start(bd_row[row:row + 1, :], rows[1:2, :]).then_inc(s_ld[12 + j], 16)

            def x_times_8(step):
                newton.done(act, step.pair())
                lo_made.done(act, step, back=2)
                for s in range(SUB):
                    c = (step.offset % 2) * SUB + s
                    a = act.activation(x8[:, step.buf, s, :], xin[:, step.pair().buf, c, :], ACT.Identity,
                                       bias=nmr8[:, step.pair().buf, c:c + 1], scale=rs8[:, step.pair().buf, c:c + 1])
                a.then_inc(x8_made.sem, 1)

            def high(step):
                x8_made.done(act, step)
                turned.done(act, step, back=2)
                stored.free(act, step)
                act.copy(xn16[:, step.buf, :, 0, :], x8[:, step.buf, :, :]).then_inc(hi_made.sem, 1)

            def move(step):
                summed.done(act, step, back=4)
                for h in range(2):
                    turned.done(act, step, h + 1)
                    act.copy(xT[:, step.offset % 4, h, :, :],
                             bank16(B_TURN + h).rearrange("p (k t) -> p k t", k=KC)).then_inc(moved.sem, 1)

            def gate(step):
                if step.offset % 2 == 0:
                    return
                pair = step.pair()
                if step.offset == 1 and isinstance(step.i, int):
                    act.wait_ge(s_prep, BIASED)
                for w in range(2):
                    half_w = slice(w * N, (w + 1) * N)
                    projected.done(act, step.plus(w - 1), 1)
                    act.activation(tanh_a[half_w, :], bank(B_AB + w)[half_w, :], ACT.Tanh, bias=ba_half[half_w, 0:1],
                                   scale=0.5 / SCALE).then_inc(gates.sem, 1)
                s_made.done(act, pair, back=2)
                cs_made.done(act, pair, back=2)
                gates.done(act, pair, 2)
                act.activation(a_sb[:, pair.buf, :], tanh_a[:, :], ACT.Identity, bias=half[:, 0:1],
                               scale=0.5).then_inc(gates.sem, 1)
                act.activation(m_sb[:, pair.buf, :], tanh_a[:, :], ACT.Identity, bias=minus_one[:, 0:1],
                               scale=1.0).then_inc(gates.sem, 1)
                for w in range(2):
                    act.activation(b_sb[w * N:(w + 1) * N, pair.buf, :], bank(B_AB + w)[(1 - w) * N:(2 - w) * N, :],
                                   ACT.Identity, bias=bb_s[w * N:(w + 1) * N, 0:1], scale=1.0).then_inc(gates.sem, 1)
                projected.done(act, step, 2)
                act.activation(c_sb[:, pair.buf, :], bank(B_C), ACT.Tanh, bias=col[:, 2:3],
                               scale=1.0 / SCALE).then_inc(gates.sem, 1)

            def w2_high(step):
                w2_in.done(act, step)
                park(act, s_mark)
                act.mul(w16[:, bass.ds(step.i + E, 1), 0:WCHUNK // 2], w_stage[:, step.buf:step.buf + 1, :],
                        W_SCALE).then_inc(w2_hi.sem, 1)

            def exponentials(step):
                if step.offset % 2:
                    route.done(act, step.pair(), CENTRED)
                    act.activation(r_exp, r_logit, ACT.Exp).then_inc(exped.sem, 1)
                    route.done(act, step.pair(), SECOND)
                    act.activation(r_exp2, r_max2, ACT.Exp).then_inc(exped.sem, 1)

            def normalize(step):
                x_times_8(step)
                high(step)

            run_steps(act, GROUPS, [(1, only(1, normalize)), (5, exponentials), (4, gate), (2, move),
                                    (1, only(0, normalize))], unroll=4)
            run_steps(act, E, [(0, w2_high)])

            weights = table[:, :, :].bitcast(F32)

            def gelu(step):
                for q in range(2):
                    hidden.done(act, step, q + 1)
                    hlo.done(act, step, q + 1, back=2)
                    act.activation(h32[step.buf][q], bank(2 * step.buf + q), ACT.Gelu,
                                   scale=1.0 / SCALE).then_inc(gelued.sem, 1)

            def weigh(step):
                y_made.done(act, step)
                put_back.free(act, step)
                fetched.done(act, step)
                park(act, s_mark)
                for s in range(TSUB):
                    y = act.mul(ys[step.buf][:, s, :], bank(4 + step.buf)[:, s * D:(s + 1) * D],
                                weights[:, bass.ds(step.i * TSUB + s, 1), 1])
                y.then_inc(y_out.sem, 1)

            run_steps(act, N_TILES, [(1, gelu), (2, weigh)], peel=4)

        @block.vector
        def _(dve):
            dve.memset(half[:, :], 0.5).then_inc(s_prep, 1)
            dve.memset(minus_one[:, :], -1.0).then_inc(s_prep, 1)
            dve.memset(eights[:, :], X_SCALE).then_inc(s_prep, 1)
            dve.memset(state[:, 1, GROUP - 1:GROUP], 0.0).then_inc(s_prep, 1)
            dve.memset(carry[:, :], 1.0).then_inc(s_prep, 1)
            dve.memset(abc16[:, :, :, :, :], 0.0).then_inc(s_prep, 1)
            dve.memset(wy16[:, :, :, :], 0.0).then_inc(s_prep, 1)
            dve.memset(one_row[:, :], 1.0).then_inc(s_prep, 1)
            dve.memset(bias16[:, :], 0.0).then_inc(s_prep, 1)
            dve.wait_ge(s_prep, 9)
            dve.memset(carry[:, ::SEQ_GROUPS], 0.0).then_inc(s_prep, 1)
            split_count = [0]

            def split(src, high_part, low_part, scale):
                dve.tensor_scalar(high_part, src, scale, None, ALU.mult).then_inc(s_small, 1)
                split_count[0] += 1
                yield partial(dve.wait_ge, s_small, split_count[0])
                dve.scalar_tensor_tensor(out=low_part, in0=src, scalar=scale, in1=high_part, op0=ALU.mult,
                                         op1=ALU.subtract).then_inc(s_small, 1)
                split_count[0] += 1

            def prepare(step):
                if step.offset != 0 or not isinstance(step.i, int):
                    return
                dve.wait_ge(s_ld[0], 16)
                dve.wait_ge(s_ld[1], 16)
                for k in range(KC):
                    dve.tensor_scalar(gated[:, k, :], gate32[:, k, :], gb[:, 0, k:k + 1], None, ALU.mult).then_inc(s_prep, 1)
                    yield
                dve.tensor_copy(beta_b[:, :, :], gb[:, 1, :].unsqueeze(2).to_broadcast([P, KC, P])).then_inc(s_betab, 1)
                dve.wait_ge(s_prep, 10 + KC)
                yield from split(gated[:, :, :], gate16[:, 0, :, :], gate16[:, 1, :, :], W_SCALE)
                assert split_count[0] == GATE_SPLIT
                for s in s_ld[2:]:
                    dve.wait_ge(s, 16)
                for w, c0, c1, at in ((0, 0, 2 * N, 0), (0, 0, N, 2 * N), (1, 2 * N, 3 * N, N)):
                    yield from split(abc32[:, :, :, :].rearrange("p k w n -> p k (w n)")[:, :, c0:c1],
                                     abc16[:, 0, :, w, at:at + c1 - c0], abc16[:, 1, :, w, at:at + c1 - c0], W_SCALE)
                yield from split(wd32[:, :, :], wd16[:, 0, :, :], wd16[:, 1, :, :], W_SCALE)
                for w in range(2):
                    rows_w = slice(w * N, (w + 1) * N)
                    yield from split(wy32[rows_w, :], wy16[rows_w, w, 0, :], wy16[rows_w, w, 1, :], W_SCALE)
                for row in (0, LOW_ROW):
                    dve.tensor_tensor(bias_row[row:row + 1, :], by_row[row:row + 1, :], bd_row[row:row + 1, :], ALU.add)\
                       .then_inc(s_prep, 1)
                    yield
                dve.tensor_scalar(bb_s[:, :], col[:, 1:2], SCALE, None, ALU.mult).then_inc(s_prep, 1)
                yield
                dve.tensor_scalar(ba_half[:, :], col[:, 0:1], 0.5, None, ALU.mult).then_inc(s_prep, 1)
                yield
                dve.wait_ge(s_prep, 14 + KC)
                dve.tensor_scalar(bias16[0:1, :], bias_row[0:1, :], W_SCALE, None, ALU.mult).then_inc(s_small, 1)
                split_count[0] += 1
                yield
                low_row = slice(LOW_ROW, LOW_ROW + 1)
                yield from split(bias_row[low_row, :], bias_high[low_row, :], bias16[low_row, :], W_SCALE)
                assert split_count[0] == ALL_SPLIT
                dve.wait_ge(s_bias8, 1)
                dve.tensor_copy(bias8[:, :], bank(B_ROUTE)[:, 0:E]).then_inc(s_prep, 1)
                yield
                assert 15 + KC == BIASED
                dve.wait_ge(s_const, 17)
                yield partial(dve.wait_ge, s_prep, BIASED)

            def take_turns(work):
                odd = any(emit is reciprocal_root and step.offset & 1 for emit, step in work)
                live = {name: chain(*(emit(step) for emit, step in work if track[emit] == name)) for name in "NRT"}
                waits = dict.fromkeys(live)
                for name in cycle("NTNR" if odd else "NRT"):
                    if name in live:
                        if waits[name] is not None:
                            waits[name]()
                        waits[name] = next(live[name], END)
                        if waits[name] is END:
                            del live[name]
                    if not live:
                        return

            def statistics(step):
                if step.offset % 2 == 0:
                    x_in.done(dve, step.pair())
                first = (step.offset % 2) * SUB
                for s in range(SUB):
                    b = dve.bn_stats(bn[:, first + s, :], xin[:, step.pair().buf, first + s, :])
                    if s == SUB - 1:
                        b.then_inc(stats.sem, 1)
                    yield
                stats.done(dve, step, 1)
                park(dve, s_mark)
                for s in range(SUB):
                    b = dve.bn_aggr(mv[:, first + s, :], bn[:, first + s, :])
                b.then_inc(stats.sem, 1)
                yield

            def reciprocal_root(step):
                if step.offset % 2 == 0:
                    return
                pair = step.pair()
                stats.done(dve, step, 2)
                count = [0]

                def then(instruction):
                    count[0] += 1
                    instruction.then_inc(newton.sem, 1)
                    return partial(newton.done, dve, pair, count[0])

                yield then(dve.tensor_scalar(ve[:, 0, :], mv[:, :, 1], EPS, None, ALU.add))
                yield then(dve.scalar_tensor_tensor(out=ve[:, 1, :], in0=ve[:, 0, :], scalar=EPS, in1=mv[:, :, 1], op0=ALU.mult,
                                              op1=ALU.add))
                yield then(dve.tensor_scalar(nh[:, :, :].bitcast(I32), ve[:, :, :].bitcast(I32), 1, None,
                                       ALU.logical_shift_right))
                yield then(dve.tensor_scalar(ny[:, :, :].bitcast(I32), nh[:, :, :].bitcast(I32), -1.0, float(MAGIC), ALU.mult,
                                       ALU.add))
                y, z = ny, nz
                for _ in range(3):
                    yield then(dve.scalar_tensor_tensor(out=nq[:, :, :], in0=y[:, :, :], scalar=-0.5, in1=y[:, :, :],
                                                  op0=ALU.mult, op1=ALU.mult))
                    yield then(dve.tensor_tensor(nq[:, :, :], nq[:, :, :], ve[:, :, :], ALU.mult))
                    yield then(dve.scalar_tensor_tensor(out=z[:, :, :], in0=nq[:, :, :], scalar=1.5, in1=y[:, :, :],
                                                  op0=ALU.add, op1=ALU.mult))
                    y, z = z, y
                yield then(dve.tensor_scalar(rs8[:, pair.buf, :], y[:, 0, :], X_SCALE, None, ALU.mult))
                yield then(dve.scalar_tensor_tensor(out=nmr8[:, pair.buf, :], in0=mv[:, :, 0], scalar=-1.0,
                                              in1=rs8[:, pair.buf, :], op0=ALU.mult, op1=ALU.mult))
                yield then(dve.tensor_tensor(root[:, :], ve[:, 0, :], y[:, 0, :], ALU.mult))
                yield then(dve.tensor_tensor(router_norm[:, bass.ds(pair.i * (2 * SUB), 2 * SUB)], root[:, :], y[:, 1, :], ALU.mult))
                assert count[0] == NEWTON

            def low(step):
                hi_made.done(dve, step)
                dve.tensor_tensor(xn16[:, step.buf, :, 1, :], x8[:, step.buf, :, :], xn16[:, step.buf, :, 0, :],
                                  ALU.subtract).then_inc(lo_made.sem, 1)
                yield

            def recur(step):
                if step.offset % 2 == 0:
                    return
                group, step = step, step.pair()
                gates.done(dve, step, 6)
                dve.tensor_tensor(u_sb[:, :], b_sb[:, step.buf, :], m_sb[:, step.buf, :], ALU.mult).then_inc(u_made.sem, 1)
                yield
                dve.tensor_tensor(initial[:, :], state[:, 1 - step.buf, GROUP - 1:GROUP], carry[:, bass.ds(step.i, 1)],
                                  ALU.mult).then_inc(init_made.sem, 1)
                yield
                u_made.done(dve, step)
                init_made.done(dve, step)
                dve.tensor_tensor_scan(state[:, step.buf, :], a_sb[:, step.buf, :], u_sb[:, :], initial[:, 0:1], ALU.mult,
                                       ALU.add).then_inc(s_made.sem, 1)
                yield
                s_made.done(dve, step)
                gates.done(dve, step, 7)
                dve.scalar_tensor_tensor(out=cs8[:, :], in0=c_sb[:, step.buf, :], scalar=-0.5 * X_SCALE / SCALE,
                                         in1=state[:, step.buf, :], op0=ALU.mult, op1=ALU.mult).then_inc(cs_made.sem, 1)
                yield
                cs_made.done(dve, step)
                summed.done(dve, group, back=4)
                dve.tensor_copy(cs16[:, step.buf, 0, :], cs8[:, :]).then_inc(cshi.sem, 1)
                yield
                cshi.done(dve, step)
                dve.tensor_tensor(cs16[:, step.buf, 1, :], cs8[:, :], cs16[:, step.buf, 0, :], ALU.subtract)\
                   .then_inc(cslo.sem, 1)
                yield

            def w2_low(step):
                w2_hi.done(dve, step)
                dve.scalar_tensor_tensor(out=w16[:, bass.ds(step.i + E, 1), WCHUNK // 2:WCHUNK],
                                         in0=w_stage[:, step.buf:step.buf + 1, :], scalar=W_SCALE,
                                         in1=w16[:, bass.ds(step.i + E, 1), 0:WCHUNK // 2], op0=ALU.mult,
                                         op1=ALU.subtract).then_inc(w2_lo.sem, 1)

            def add_x(step):
                x_again.done(dve, step)
                out_put.free(dve, step)
                for j in range(2):
                    summed.done(dve, step, j + 1)
                    s = 2 * j
                    dve.scalar_tensor_tensor(out=out_sb[:, step.buf, s:s + 2, :].rearrange("p s d -> p (s d)"),
                                             in0=bank(B_SUM + j), scalar=1.0 / SCALE,
                                             in1=x_res[:, step.buf, s:s + 2, :].rearrange("p s d -> p (s d)"),
                                             op0=ALU.mult, op1=ALU.add).then_inc(added.sem, 1)
                    yield

            steps = [0]

            def by_e(ap):
                return ap.unsqueeze(2).to_broadcast([P, BT, E])

            def to_e(ap):
                return ap.unsqueeze(1).to_broadcast([P, BT, E])

            def te(ap):
                return ap.rearrange("p (t e) -> p t e", e=E)

            def counter(batch):
                def then(instruction, name=None):
                    steps[0] += 1
                    instruction.then_inc(route.sem, 1)
                    if name is not None:
                        assert steps[0] == name, (steps[0], name)
                    return partial(route.done, dve, batch, steps[0])
                return then

            def centre(step):
                if step.offset % 2 == 0:
                    return
                steps[0] = 0
                then = counter(step.pair())
                scored.done(dve, step)
                logit = te(r_logit)
                products = bank(B_ROUTE)[:, SCORE_COL:SCORE_COL + BT * E]
                norm = router_norm[:, bass.ds(step.pair().i * BT, BT)]
                yield then(dve.scalar_tensor_tensor(out=logit, in0=te(products), scalar=1.0 / SCALE,
                                              in1=by_e(norm), op0=ALU.mult, op1=ALU.mult), LOGITS)
                yield then(dve.tensor_tensor(logit, logit, to_e(bias8[:, :]), ALU.add))
                yield then(dve.tensor_reduce(r_max1, logit, AX.X, ALU.max))
                yield then(dve.tensor_tensor(logit, logit, by_e(r_max1), ALU.subtract), CENTRED)

            def pick(step):
                if step.offset % 2 == 0:
                    return
                steps[0] = CENTRED
                then = counter(step.pair())
                logit, rest = te(r_logit), te(r_rest)

                def choose(src, top, one_hot):
                    v = te(r_tmp)
                    if top is None:
                        yield then(dve.scalar_tensor_tensor(out=v, in0=src, scalar=0.0, in1=to_e(rank[:, :]),
                                                      op0=ALU.is_equal, op1=ALU.mult))
                    else:
                        yield then(dve.tensor_tensor(v, src, by_e(top), ALU.is_equal))
                        yield then(dve.tensor_tensor(v, v, to_e(rank[:, :]), ALU.mult))
                    yield then(dve.tensor_reduce(r_rank, v, AX.X, ALU.max))
                    yield then(dve.tensor_tensor(te(one_hot), v, by_e(r_rank), ALU.is_equal))

                yield from choose(logit, None, r_one1)
                yield then(dve.scalar_tensor_tensor(out=r_rest, in0=r_one1, scalar=-1e30, in1=r_logit, op0=ALU.mult,
                                              op1=ALU.add))
                yield then(dve.tensor_reduce(r_max2, rest, AX.X, ALU.max), SECOND)
                yield from choose(rest, r_max2, r_one2)
                yield then(dve.tensor_tensor(chosen16[:, :], r_one1, r_one2, ALU.add), CHOSEN)

            def place_pairs(step):
                if step.offset % 2 == 0:
                    return
                steps[0] = CHOSEN
                then = counter(step.pair())
                counted.done(dve, step.pair())
                run = r_run.rearrange("p (e t) -> p e t", e=E)
                yield then(dve.tensor_copy(r_tot.rearrange("p (e t) -> p e t", e=E),
                                     bank(B_ROUTE)[:, COUNT_COL + BT * E:COUNT_COL + 2 * BT * E].rearrange("p (t e) -> p e t", e=E)))
                yield then(dve.tensor_tensor(te(r_slot), te(bank(B_ROUTE)[:, COUNT_COL:COUNT_COL + BT * E]),
                                             to_e(next_row[:, :]), ALU.add), COUNTS_READ)
                yield then(dve.tensor_tensor_scan(r_run, keep[:, :, :].rearrange("p e t -> p (e t)"), r_tot, 0.0, ALU.mult,
                                                  ALU.add))
                yield then(dve.tensor_tensor(r_tot, r_run, r_tot, ALU.subtract))
                yield then(dve.tensor_tensor(te(r_slot), te(r_slot), r_tot.rearrange("p (e t) -> p t e", e=E), ALU.add))
                yield then(dve.tensor_tensor(next_row[:, :], next_row[:, :], run[:, :, BT - 1], ALU.add))
                buf = step.pair().buf
                for j, one in enumerate((r_one1, r_one2)):
                    yield then(dve.tensor_tensor(r_tmp, one, r_slot, ALU.mult))
                    yield then(dve.tensor_reduce(r_row[:, j * BT:(j + 1) * BT], te(r_tmp), AX.X, ALU.add))
                spread.done(dve, step.pair(), back=2)
                yield then(dve.tensor_copy(pair_row[:, buf, :], r_row[:, :]), PLACED)
            def weigh_pairs(step):
                if step.offset % 2 == 0:
                    return
                steps[0] = PLACED
                then = counter(step.pair())
                exped.done(dve, step.pair())
                yield then(dve.tensor_reduce(r_sum, te(r_exp), AX.X, ALU.add))
                buf = step.pair().buf
                pair_weight = pair_val[:, :, :, :].bitcast(F32)[:, buf, :, :]
                yield then(dve.reciprocal(r_rank, r_sum))
                dve.tensor_scalar(pair_weight[:, 0:BT, 1], r_rank, 1.0 / SCALE, None, ALU.mult)
                yield then(dve.scalar_tensor_tensor(out=pair_weight[:, BT:2 * BT, 1], in0=r_exp2, scalar=1.0 / SCALE,
                                              in1=r_rank, op0=ALU.mult, op1=ALU.mult))
                yield then(dve.tensor_scalar(pair_val[:, buf, :, 0], pair_val[:, buf, :, 0], float(2 * GROUP), None,
                                             ALU.add), ROUTED)

            track = {statistics: "N", reciprocal_root: "N", low: "R", recur: "R", add_x: "R", prepare: "R",
                     centre: "T", pick: "T", place_pairs: "T", weigh_pairs: "T"}
            run_steps(dve, GROUPS, [(0, statistics), (0, reciprocal_root), (2, low), (6, add_x), (4, recur), (1, prepare),
                                    (4, centre), (4, pick), (5, place_pairs), (5, weigh_pairs)],
                      unroll=4, emit_step=take_turns)

            w2_low(Step(0, 0))
            w2_low(Step(0, 1))

            planned = [0]

            def plan(instruction):
                planned[0] += 1
                instruction.then_inc(s_plan, 1)
                dve.wait_ge(s_plan, planned[0])

            plan(dve.tensor_tensor(r_cnt, next_row[0:1, :], list_start[0:1, :], ALU.subtract))
            plan(dve.tensor_scalar(r_int, r_cnt, float(TILE - 1), None, ALU.add))
            plan(dve.tensor_scalar(r_int2, r_int, TILE.bit_length() - 1, None, ALU.logical_shift_right))
            plan(dve.tensor_copy(r_tiles, r_int2))
            plan(dve.tensor_tensor_scan(r_end, one_row[:, :], r_tiles, 0.0, ALU.mult, ALU.add))
            ends = r_end[0:1, 0:E - 1].unsqueeze(1).to_broadcast([1, N_TILES, E - 1])
            plan(dve.tensor_tensor(r_cmp[:, :, :], tile_no[0:1, :].unsqueeze(2).to_broadcast([1, N_TILES, E - 1]), ends,
                                   ALU.is_ge))
            plan(dve.tensor_reduce(r_te[:, :], r_cmp[:, :, :], AX.X, ALU.add))
            plan(dve.tensor_tensor(r_cmp[:, :, :], r_cmp[:, :, :], ends, ALU.mult))
            plan(dve.tensor_reduce(r_first[:, :], r_cmp[:, :, :], AX.X, ALU.max))
            plan(dve.tensor_scalar(expert_off[:, :], r_te[:, :], float(WCHUNK), None, ALU.mult))
            plan(dve.tensor_tensor(r_first[:, :], tile_no[:, :], r_first[:, :], ALU.subtract))
            plan(dve.tensor_scalar(r_off[:, :], r_te[:, :], float(TOKENS), None, ALU.mult))
            plan(dve.scalar_tensor_tensor(out=tile_row[:, :], in0=r_first[:, :], scalar=float(TILE), in1=r_off[:, :],
                                          op0=ALU.mult, op1=ALU.add))
            assert planned[0] == PLANNED

            run_steps(dve, E - 2, [(0, lambda step: w2_low(step.plus(2)))])

            def g_move(step):
                g_turned.done(dve, step)
                hidden.done(dve, step, back=2)
                for h in range(2):
                    dve.tensor_copy(tT[step.buf][:, h, :, :].rearrange("p k t -> p (k t)"),
                                    bank16(6 + step.buf)[:, h * KC * TILE:(h + 1) * KC * TILE])\
                       .then_inc(g_moved.sem, 1)

            def h_split(step):
                for q in range(2):
                    gelued.done(dve, step, q + 1)
                    if q == 0:
                        y_made.done(dve, step, back=2)
                    high_part = h16[step.buf][:, 0, 2 * q:2 * q + 2, :].rearrange("p f t -> p (f t)")
                    low_part = h16[step.buf][:, 1, 2 * q:2 * q + 2, :].rearrange("p f t -> p (f t)")
                    dve.tensor_scalar(high_part, h32[step.buf][q], X_SCALE, None, ALU.mult).then_inc(hhi.sem, 1)
                    hhi.done(dve, step, q + 1)
                    dve.scalar_tensor_tensor(out=low_part, in0=h32[step.buf][q], scalar=X_SCALE, in1=high_part,
                                             op0=ALU.mult, op1=ALU.subtract).then_inc(hlo.sem, 1)

            run_steps(dve, N_TILES, [(0, g_move), (1, h_split)])


def kernel(**inputs):
    import numpy as np
    import concourse.bacc as bacc
    from concourse.bass_utils import run_bass_kernel_spmd

    def arr(name):
        return np.asarray(inputs[name])

    w1 = arr("L0_ffn_w1").reshape(E, F, KC, P).transpose(3, 0, 2, 1).reshape(P, E, KC * F)
    w2 = arr("L0_ffn_w2").reshape(E, D, FC, P).transpose(3, 0, 2, 1).reshape(P, E, FC * D)
    laid_out = {
        "x": arr("L0_attn_x"), "wa": arr("L0_attn_Wa"), "wb": arr("L0_attn_Wb"), "wc": arr("L0_attn_Wc"),
        "wd": arr("L0_attn_Wd"), "wy": arr("L0_attn_Wy"),
        "cols": np.stack([arr("L0_attn_ba"), arr("L0_attn_bb"), arr("L0_attn_bc")], axis=1),
        "rows": np.stack([arr("L0_attn_by"), arr("L0_attn_bd")]),
        "gate": arr("L0_ffn_gate_w").reshape(E, KC, P).transpose(2, 1, 0),
        "gamma_beta": np.stack([arr("L0_ffn_ln_gamma"), arr("L0_ffn_ln_beta")]).reshape(2, KC, P).transpose(2, 0, 1),
        "experts": np.concatenate([w1, w2], axis=1),
    }
    nc = bacc.Bacc("TRN2", target_bir_lowering=False, num_devices=1)
    arrays, args = {}, []
    for name, a in laid_out.items():
        a = np.ascontiguousarray(a)
        arrays[f"in_{name}"] = a
        args.append(nc.dram_tensor(f"in_{name}", a.shape, mybir.dt.from_np(a.dtype), kind="ExternalInput").ap())
    args.append(nc.dram_tensor("out_0", (BATCH, SEQ, D), F32, kind="ExternalOutput").ap())
    build(nc, *args)
    return run_bass_kernel_spmd(nc, [arrays], core_ids=[0]).results[0]["out_0"]
```
